# Optimizing a Trainium2 kernel written in Bass

```python
import numpy as np
import jax
import jax.numpy as jnp

def _softmax(x, axis=-1):
    return jax.nn.softmax(x, axis=axis)

def _gelu(x):
    return jax.nn.gelu(x, approximate=True)

def _silu(x):
    return jax.nn.silu(x)

def _sigmoid(x):
    return jax.nn.sigmoid(x)

def _layernorm(x, axis=-1, eps=1e-05):
    m = jnp.mean(x, axis=axis, keepdims=True)
    v = jnp.var(x, axis=axis, keepdims=True)
    return (x - m) / jnp.sqrt(v + eps)

def _scatter_add(tgt, idx, src, axis=0):
    return tgt.at[idx].add(src)

def _segment_sum(src, seg, n):
    return jax.ops.segment_sum(src, seg, n)
kernel_name = 'mk_seq_preln_d2_jaxref_r4_711fb6'

def setup_inputs(seed: int=0):
    np.random.seed(seed)
    _w = jnp.asarray

    def _L0_attn_setup():
        import jax, jax.numpy as jnp
        import numpy as np
        N_HEADS = 16

        def _alibi_causal_mask(T, n_heads, dtype):
            slopes = (1.0 / jnp.power(2.0, jnp.arange(1, n_heads + 1, dtype=dtype)))[:, None, None]
            idx = jnp.arange(T)
            rel = (idx[None, :] - idx[:, None]).astype(dtype)
            alibi = jnp.tril(rel)
            causal = jnp.where(idx[None, :] > idx[:, None], -jnp.inf, 0.0).astype(dtype)
            return (alibi + causal)[None, :, :] * slopes
        key = jax.random.key(seed)
        ks = jax.random.split(key, 5)
        B, T, C = (2, 512, 256)
        scale = 0.02
        return {'x': jax.random.normal(ks[0], (B, T, C), dtype=jnp.float32), 'W_attn': jax.random.normal(ks[1], (C, 3 * C), dtype=jnp.float32) * scale, 'b_attn': jax.random.normal(ks[2], (3 * C,), dtype=jnp.float32) * scale, 'W_proj': jax.random.normal(ks[3], (C, C), dtype=jnp.float32) * scale, 'b_proj': jax.random.normal(ks[4], (C,), dtype=jnp.float32) * scale}
    _L0_attn_in = _L0_attn_setup()

    def _L0_ffn_setup():
        import jax, jax.numpy as jnp
        import numpy as np
        DIM = 256
        DEPTH = 2
        HEADS = 8
        DIM_HEAD = 64
        WINDOW = 128
        INNER = HEADS * DIM_HEAD
        HID = int(DIM * 4 * 2 / 3)
        B, N = (2, 2048)
        QK_SCALE = 8.0

        def shift_token(t):
            t1, t2 = jnp.split(t, 2, axis=-1)
            t2 = jnp.pad(t2, ((0, 0), (1, 0), (0, 0)))[:, :-1]
            return jnp.concatenate([t1, t2], axis=-1)

        def l2norm(t):
            return t / jnp.clip(jnp.linalg.norm(t, axis=-1, keepdims=True), 1e-12)

        def rotate_half(x):
            x1, x2 = jnp.split(x, 2, axis=-1)
            return jnp.concatenate([-x2, x1], axis=-1)

        def rotary_xpos(q, k):
            n = q.shape[-2]
            half_idx = jnp.arange(0, DIM_HEAD, 2, dtype=jnp.float32)
            inv_freq = 1.0 / 10000.0 ** (half_idx / DIM_HEAD)
            t = jnp.arange(n, dtype=jnp.float32)
            freqs = t[:, None] * inv_freq[None, :]
            freqs = jnp.concatenate([freqs, freqs], axis=-1)
            base = (half_idx + 0.4 * DIM_HEAD) / (1.4 * DIM_HEAD)
            power = (t - n // 2) / float(WINDOW // 2)
            scale = base[None, :] ** power[:, None]
            scale = jnp.concatenate([scale, scale], axis=-1)
            cos, sin = (jnp.cos(freqs), jnp.sin(freqs))
            q = q * cos * scale + rotate_half(q) * sin * scale
            k = k * cos / scale + rotate_half(k) * sin / scale
            return (q, k)

        def local_attention(q, k, v):
            b, h, n, d = q.shape
            w = n // WINDOW
            bq = q.reshape(b, h, w, WINDOW, d) * QK_SCALE
            bk = k.reshape(b, h, w, WINDOW, d)
            bv = v.reshape(b, h, w, WINDOW, d)

            def look_around(t):
                p = jnp.pad(t, ((0, 0), (0, 0), (1, 0), (0, 0), (0, 0)))
                return jnp.concatenate([p[:, :, :w], p[:, :, 1:]], axis=3)
            bk, bv = (look_around(bk), look_around(bv))
            bt = jnp.arange(n).reshape(w, WINDOW)
            btp = jnp.pad(bt, ((1, 0), (0, 0)), constant_values=-1)
            btk = jnp.concatenate([btp[:w], btp[1:]], axis=1)
            sim = jnp.einsum('bhwid,bhwjd->bhwij', bq, bk)
            i = bt[:, :, None]
            j = btk[:, None, :]
            mask = (i < j) | (i > j + WINDOW) | (j == -1)
            sim = jnp.where(mask, -jnp.finfo(sim.dtype).max, sim)
            attn = jax.nn.softmax(sim, axis=-1)
            out = jnp.einsum('bhwij,bhwjd->bhwid', attn, bv)
            return out.reshape(b, h, n, d)

        def _layer(x, wqkv, qs, ksc, wo, lg, lb, w1, b1, w2, b2):
            b, n, _ = x.shape
            h = shift_token(x)
            qkv = h @ wqkv
            q, k, v = jnp.split(qkv, 3, axis=-1)
            to_heads = lambda t: t.reshape(b, n, HEADS, DIM_HEAD).transpose(0, 2, 1, 3)
            q, k, v = (to_heads(q), to_heads(k), to_heads(v))
            q = l2norm(q) * qs
            k = l2norm(k) * ksc
            q, k = rotary_xpos(q, k)
            o = local_attention(q, k, v)
            o = o.transpose(0, 2, 1, 3).reshape(b, n, INNER)
            x = x + o @ wo
            h = shift_token(x)
            mu = h.mean(-1, keepdims=True)
            var = h.var(-1, keepdims=True)
            h = (h - mu) / jnp.sqrt(var + 1e-05) * lg + lb
            h = h @ w1 + b1
            a, g = jnp.split(h, 2, axis=-1)
            h = a * jax.nn.gelu(g, approximate=False)
            x = x + h @ w2 + b2
            return x
        key = jax.random.key(seed)
        ks = jax.random.split(key, 6)
        return {'x': jax.random.normal(ks[0], (B, N, DIM), jnp.float32), 'wqkv': jax.random.normal(ks[1], (DEPTH, DIM, 3 * INNER), jnp.float32) * 0.02, 'q_scale': jnp.ones((DEPTH, DIM_HEAD), jnp.float32), 'k_scale': jnp.ones((DEPTH, DIM_HEAD), jnp.float32), 'wo': jax.random.normal(ks[2], (DEPTH, INNER, DIM), jnp.float32) * 0.02, 'ln_g': jnp.ones((DEPTH, DIM), jnp.float32), 'ln_b': jnp.zeros((DEPTH, DIM), jnp.float32), 'w1': jax.random.normal(ks[3], (DEPTH, DIM, 2 * HID), jnp.float32) * 0.02, 'b1': jnp.zeros((DEPTH, 2 * HID), jnp.float32), 'w2': jax.random.normal(ks[4], (DEPTH, HID, DIM), jnp.float32) * 0.02, 'b2': jnp.zeros((DEPTH, DIM), jnp.float32)}
    _L0_ffn_in = _L0_ffn_setup()

    def _L1_attn_setup():
        import jax, jax.numpy as jnp
        import numpy as np
        B, L, D_MODEL = (2, 512, 256)
        D_STATE, EXPAND, D_CONV = (16, 2, 4)
        D_INNER = EXPAND * D_MODEL
        DT_RANK = D_MODEL // 16
        key = jax.random.key(seed)
        ks = jax.random.split(key, 8)
        s = lambda k, sh, sc: jax.random.normal(k, sh, dtype=jnp.float32) * sc
        return {'hidden_states': s(ks[0], (B, L, D_MODEL), 1.0), 'W_in': s(ks[1], (D_MODEL, 2 * D_INNER), D_MODEL ** (-0.5)), 'conv_w': s(ks[2], (D_CONV, D_INNER), 0.2), 'conv_b': jnp.zeros((D_INNER,), jnp.float32), 'W_x': s(ks[3], (D_INNER, DT_RANK + 2 * D_STATE), D_INNER ** (-0.5)), 'W_dt': s(ks[4], (DT_RANK, D_INNER), DT_RANK ** (-0.5)), 'b_dt': jnp.full((D_INNER,), -4.0) + s(ks[5], (D_INNER,), 0.1), 'A_log': jnp.log(jnp.broadcast_to(jnp.arange(1, D_STATE + 1, dtype=jnp.float32), (D_INNER, D_STATE))), 'D': jnp.ones((D_INNER,), jnp.float32), 'W_out': s(ks[6], (D_INNER, D_MODEL), D_INNER ** (-0.5))}
    _L1_attn_in = _L1_attn_setup()

    def _L1_ffn_setup():
        import math
        import jax, jax.numpy as jnp
        import numpy as np
        CAPACITY_FACTOR = 1.25
        key = jax.random.key(seed)
        ks = jax.random.split(key, 5)
        B, S, H, F, E = (4, 1024, 256, 256, 32)
        scale_in = 1.0 / math.sqrt(H)
        scale_mid = 1.0 / math.sqrt(F)
        return {'x': jax.random.normal(ks[0], (B, S, H), dtype=jnp.float32), 'w_router': jax.random.normal(ks[1], (H, E), dtype=jnp.float32) * scale_in, 'w_gate': jax.random.normal(ks[2], (E, H, F), dtype=jnp.float32) * scale_in, 'w_up': jax.random.normal(ks[3], (E, H, F), dtype=jnp.float32) * scale_in, 'w_down': jax.random.normal(ks[4], (E, F, H), dtype=jnp.float32) * scale_mid}
    _L1_ffn_in = _L1_ffn_setup()
    _d = {'L0_attn_x': _L0_attn_in['x'], 'L0_attn_W_attn': _L0_attn_in['W_attn'], 'L0_attn_b_attn': _L0_attn_in['b_attn'], 'L0_attn_W_proj': _L0_attn_in['W_proj'], 'L0_attn_b_proj': _L0_attn_in['b_proj'], 'L0_ffn_wqkv': _L0_ffn_in['wqkv'], 'L0_ffn_q_scale': _L0_ffn_in['q_scale'], 'L0_ffn_k_scale': _L0_ffn_in['k_scale'], 'L0_ffn_wo': _L0_ffn_in['wo'], 'L0_ffn_ln_g': _L0_ffn_in['ln_g'], 'L0_ffn_ln_b': _L0_ffn_in['ln_b'], 'L0_ffn_w1': _L0_ffn_in['w1'], 'L0_ffn_b1': _L0_ffn_in['b1'], 'L0_ffn_w2': _L0_ffn_in['w2'], 'L0_ffn_b2': _L0_ffn_in['b2'], 'L1_attn_W_in': _L1_attn_in['W_in'], 'L1_attn_conv_w': _L1_attn_in['conv_w'], 'L1_attn_conv_b': _L1_attn_in['conv_b'], 'L1_attn_W_x': _L1_attn_in['W_x'], 'L1_attn_W_dt': _L1_attn_in['W_dt'], 'L1_attn_b_dt': _L1_attn_in['b_dt'], 'L1_attn_A_log': _L1_attn_in['A_log'], 'L1_attn_D': _L1_attn_in['D'], 'L1_attn_W_out': _L1_attn_in['W_out'], 'L1_ffn_w_router': _L1_ffn_in['w_router'], 'L1_ffn_w_gate': _L1_ffn_in['w_gate'], 'L1_ffn_w_up': _L1_ffn_in['w_up'], 'L1_ffn_w_down': _L1_ffn_in['w_down']}
    _x0 = _d['L0_attn_x']
    _d['L0_attn_x'] = jax.random.normal(jax.random.fold_in(jax.random.key(seed), 1), (4, 1024, 256), dtype=_x0.dtype)
    del _x0
    return _d

def reference(L0_attn_x, L0_attn_W_attn, L0_attn_b_attn, L0_attn_W_proj, L0_attn_b_proj, L0_ffn_wqkv, L0_ffn_q_scale, L0_ffn_k_scale, L0_ffn_wo, L0_ffn_ln_g, L0_ffn_ln_b, L0_ffn_w1, L0_ffn_b1, L0_ffn_w2, L0_ffn_b2, L1_attn_W_in, L1_attn_conv_w, L1_attn_conv_b, L1_attn_W_x, L1_attn_W_dt, L1_attn_b_dt, L1_attn_A_log, L1_attn_D, L1_attn_W_out, L1_ffn_w_router, L1_ffn_w_gate, L1_ffn_w_up, L1_ffn_w_down):

    def _L0_attn_ref(x, W_attn, b_attn, W_proj, b_proj):
        import jax, jax.numpy as jnp
        import numpy as np
        N_HEADS = 16

        def _alibi_causal_mask(T, n_heads, dtype):
            slopes = (1.0 / jnp.power(2.0, jnp.arange(1, n_heads + 1, dtype=dtype)))[:, None, None]
            idx = jnp.arange(T)
            rel = (idx[None, :] - idx[:, None]).astype(dtype)
            alibi = jnp.tril(rel)
            causal = jnp.where(idx[None, :] > idx[:, None], -jnp.inf, 0.0).astype(dtype)
            return (alibi + causal)[None, :, :] * slopes
        B, T, C = x.shape
        H = N_HEADS
        D = C // H
        qkv = x @ W_attn + b_attn
        q, k, v = jnp.split(qkv, 3, axis=-1)
        q = q.reshape(B, T, H, D).transpose(0, 2, 1, 3)
        k = k.reshape(B, T, H, D).transpose(0, 2, 1, 3)
        v = v.reshape(B, T, H, D).transpose(0, 2, 1, 3)
        att = jnp.einsum('bhtd,bhsd->bhts', q, k) / jnp.sqrt(jnp.asarray(D, x.dtype))
        att = att + _alibi_causal_mask(T, H, x.dtype)[None]
        att = jax.nn.softmax(att, axis=-1)
        y = jnp.einsum('bhts,bhsd->bhtd', att, v)
        y = y.transpose(0, 2, 1, 3).reshape(B, T, C)
        return y @ W_proj + b_proj

    def _L0_ffn_ref(x, wqkv, q_scale, k_scale, wo, ln_g, ln_b, w1, b1, w2, b2):
        import jax, jax.numpy as jnp
        import numpy as np
        DIM = 256
        DEPTH = 2
        HEADS = 8
        DIM_HEAD = 64
        WINDOW = 128
        INNER = HEADS * DIM_HEAD
        HID = int(DIM * 4 * 2 / 3)
        B, N = (2, 2048)
        QK_SCALE = 8.0

        def shift_token(t):
            t1, t2 = jnp.split(t, 2, axis=-1)
            t2 = jnp.pad(t2, ((0, 0), (1, 0), (0, 0)))[:, :-1]
            return jnp.concatenate([t1, t2], axis=-1)

        def l2norm(t):
            return t / jnp.clip(jnp.linalg.norm(t, axis=-1, keepdims=True), 1e-12)

        def rotate_half(x):
            x1, x2 = jnp.split(x, 2, axis=-1)
            return jnp.concatenate([-x2, x1], axis=-1)

        def rotary_xpos(q, k):
            n = q.shape[-2]
            half_idx = jnp.arange(0, DIM_HEAD, 2, dtype=jnp.float32)
            inv_freq = 1.0 / 10000.0 ** (half_idx / DIM_HEAD)
            t = jnp.arange(n, dtype=jnp.float32)
            freqs = t[:, None] * inv_freq[None, :]
            freqs = jnp.concatenate([freqs, freqs], axis=-1)
            base = (half_idx + 0.4 * DIM_HEAD) / (1.4 * DIM_HEAD)
            power = (t - n // 2) / float(WINDOW // 2)
            scale = base[None, :] ** power[:, None]
            scale = jnp.concatenate([scale, scale], axis=-1)
            cos, sin = (jnp.cos(freqs), jnp.sin(freqs))
            q = q * cos * scale + rotate_half(q) * sin * scale
            k = k * cos / scale + rotate_half(k) * sin / scale
            return (q, k)

        def local_attention(q, k, v):
            b, h, n, d = q.shape
            w = n // WINDOW
            bq = q.reshape(b, h, w, WINDOW, d) * QK_SCALE
            bk = k.reshape(b, h, w, WINDOW, d)
            bv = v.reshape(b, h, w, WINDOW, d)

            def look_around(t):
                p = jnp.pad(t, ((0, 0), (0, 0), (1, 0), (0, 0), (0, 0)))
                return jnp.concatenate([p[:, :, :w], p[:, :, 1:]], axis=3)
            bk, bv = (look_around(bk), look_around(bv))
            bt = jnp.arange(n).reshape(w, WINDOW)
            btp = jnp.pad(bt, ((1, 0), (0, 0)), constant_values=-1)
            btk = jnp.concatenate([btp[:w], btp[1:]], axis=1)
            sim = jnp.einsum('bhwid,bhwjd->bhwij', bq, bk)
            i = bt[:, :, None]
            j = btk[:, None, :]
            mask = (i < j) | (i > j + WINDOW) | (j == -1)
            sim = jnp.where(mask, -jnp.finfo(sim.dtype).max, sim)
            attn = jax.nn.softmax(sim, axis=-1)
            out = jnp.einsum('bhwij,bhwjd->bhwid', attn, bv)
            return out.reshape(b, h, n, d)

        def _layer(x, wqkv, qs, ksc, wo, lg, lb, w1, b1, w2, b2):
            b, n, _ = x.shape
            h = shift_token(x)
            qkv = h @ wqkv
            q, k, v = jnp.split(qkv, 3, axis=-1)
            to_heads = lambda t: t.reshape(b, n, HEADS, DIM_HEAD).transpose(0, 2, 1, 3)
            q, k, v = (to_heads(q), to_heads(k), to_heads(v))
            q = l2norm(q) * qs
            k = l2norm(k) * ksc
            q, k = rotary_xpos(q, k)
            o = local_attention(q, k, v)
            o = o.transpose(0, 2, 1, 3).reshape(b, n, INNER)
            x = x + o @ wo
            h = shift_token(x)
            mu = h.mean(-1, keepdims=True)
            var = h.var(-1, keepdims=True)
            h = (h - mu) / jnp.sqrt(var + 1e-05) * lg + lb
            h = h @ w1 + b1
            a, g = jnp.split(h, 2, axis=-1)
            h = a * jax.nn.gelu(g, approximate=False)
            x = x + h @ w2 + b2
            return x
        for l in range(DEPTH):
            x = _layer(x, wqkv[l], q_scale[l], k_scale[l], wo[l], ln_g[l], ln_b[l], w1[l], b1[l], w2[l], b2[l])
        return x

    def _L1_attn_ref(hidden_states, W_in, conv_w, conv_b, W_x, W_dt, b_dt, A_log, D, W_out):
        import jax, jax.numpy as jnp
        import numpy as np
        B, L, D_MODEL = (2, 512, 256)
        D_STATE, EXPAND, D_CONV = (16, 2, 4)
        D_INNER = EXPAND * D_MODEL
        DT_RANK = D_MODEL // 16
        silu = jax.nn.silu
        xz = hidden_states @ W_in
        x, z = jnp.split(xz, 2, axis=-1)
        x = jax.lax.conv_general_dilated(x, conv_w[:, None, :], (1,), [(D_CONV - 1, 0)], dimension_numbers=('NWC', 'WIO', 'NWC'), feature_group_count=D_INNER)
        x = silu(x + conv_b)
        proj = x @ W_x
        dt_low = proj[..., :DT_RANK]
        Bm = proj[..., DT_RANK:DT_RANK + D_STATE]
        Cm = proj[..., DT_RANK + D_STATE:]
        dt = jax.nn.softplus(dt_low @ W_dt + b_dt)
        A = -jnp.exp(A_log)

        def step(h, inputs):
            dt_t, x_t, B_t, C_t = inputs
            h = jnp.exp(dt_t[..., None] * A) * h + (dt_t * x_t)[..., None] * B_t[:, None, :]
            y = jnp.einsum('bds,bs->bd', h, C_t)
            return (h, y)
        h0 = jnp.zeros((hidden_states.shape[0], D_INNER, D_STATE), x.dtype)
        xs = (jnp.swapaxes(dt, 0, 1), jnp.swapaxes(x, 0, 1), jnp.swapaxes(Bm, 0, 1), jnp.swapaxes(Cm, 0, 1))
        _, ys = jax.lax.scan(step, h0, xs)
        y = jnp.swapaxes(ys, 0, 1) + x * D
        y = y * silu(z)
        return y @ W_out

    def _L1_ffn_ref(x, w_router, w_gate, w_up, w_down):
        import math
        import jax, jax.numpy as jnp
        import numpy as np
        CAPACITY_FACTOR = 1.25
        B, S, H = x.shape
        E = w_gate.shape[0]
        T = B * S
        C = int(math.ceil(CAPACITY_FACTOR * T / E))
        xt = x.reshape(T, H)
        logits = xt @ w_router
        probs = jax.nn.softmax(logits, axis=-1)
        top1 = jnp.argmax(probs, axis=-1)
        gate = jnp.take_along_axis(probs, top1[:, None], axis=1)[:, 0]
        onehot = jax.nn.one_hot(top1, E, dtype=jnp.int32)
        pos = jnp.cumsum(onehot, axis=0)[jnp.arange(T), top1] - 1
        accepted = pos < C
        slot = jnp.where(accepted, top1 * C + pos, E * C)
        buf = jnp.zeros((E * C + 1, H), dtype=x.dtype).at[slot].set(xt)
        buf = buf[:E * C].reshape(E, C, H)
        g = jnp.einsum('ech,ehf->ecf', buf, w_gate)
        u = jnp.einsum('ech,ehf->ecf', buf, w_up)
        y = jnp.einsum('ecf,efh->ech', jax.nn.silu(g) * u, w_down)
        out_tok = y.reshape(E * C, H)[jnp.clip(slot, 0, E * C - 1)]
        out_tok = jnp.where(accepted[:, None], out_tok * gate[:, None], 0.0)
        return (xt + out_tok).reshape(B, S, H)
    x = L0_attn_x
    x = x + _L0_attn_ref(_layernorm(x, axis=-1), L0_attn_W_attn, L0_attn_b_attn, L0_attn_W_proj, L0_attn_b_proj)
    x = x + _L0_ffn_ref(_layernorm(x, axis=-1), L0_ffn_wqkv, L0_ffn_q_scale, L0_ffn_k_scale, L0_ffn_wo, L0_ffn_ln_g, L0_ffn_ln_b, L0_ffn_w1, L0_ffn_b1, L0_ffn_w2, L0_ffn_b2)
    x = x + _L1_attn_ref(_layernorm(x, axis=-1), L1_attn_W_in, L1_attn_conv_w, L1_attn_conv_b, L1_attn_W_x, L1_attn_W_dt, L1_attn_b_dt, L1_attn_A_log, L1_attn_D, L1_attn_W_out)
    x = x + _L1_ffn_ref(_layernorm(x, axis=-1), L1_ffn_w_router, L1_ffn_w_gate, L1_ffn_w_up, L1_ffn_w_down)
    return x

_drawn_inputs = setup_inputs


def setup_inputs(seed=0):
    import zlib

    import numpy as np

    out = dict(_drawn_inputs(seed))
    spreads = {'L0_ffn_q_scale': (1.0, 0.6),
     'L0_ffn_k_scale': (1.0, 0.6),
     'L0_ffn_ln_g': (1.0, 0.6),
     'L0_ffn_ln_b': (0.0, 0.8),
     'L0_ffn_b1': (0.0, 0.771),
     'L0_ffn_b2': (0.0, 0.1),
     'L1_attn_conv_b': (0.0, 0.461),
     'L1_attn_D': (1.0, 0.6)}
    factors = {'L0_attn_W_attn': 2.819,
     'L0_attn_b_attn': 7.197,
     'L0_attn_b_proj': 2.822,
     'L0_ffn_wqkv': 3.274,
     'L0_ffn_wo': 3.187,
     'L1_attn_W_x': 8.0,
     'L1_attn_W_dt': 8.0,
     'L1_attn_b_dt': 8.0,
     'L1_attn_A_log': 8.0,
     'L1_ffn_w_router': 8.0,
     'L1_ffn_w_gate': 8.0,
     'L1_ffn_w_up': 8.0,
     'L1_ffn_w_down': 8.0}
    for name, (base, spread) in spreads.items():
        noise = np.random.default_rng([zlib.crc32(name.encode()), seed]).standard_normal(out[name].shape)
        drawn = base * np.exp(spread * noise) if base else spread * noise
        out[name] = jnp.asarray(drawn.astype(out[name].dtype))
    for name, factor in factors.items():
        out[name] = (out[name] * factor).astype(out[name].dtype)
    return out
```

```python
from contextlib import ExitStack

import numpy as np
import concourse.bass as bass
from concourse import mybir
from concourse.alu_op_type import AluOpType as ALU

ACT = mybir.ActivationFunctionType
AX = mybir.AxisListType
F32 = mybir.dt.float32
BF16 = mybir.dt.bfloat16
I32 = mybir.dt.int32
U32 = mybir.dt.uint32

P = 128
SEQS, SEQ, DIM = 4, 1024, 256
TOKENS = SEQS * SEQ
TILES = TOKENS // P
CHUNK = 512
CHUNKS = TOKENS // CHUNK
CT = CHUNK // P
KD = DIM // P
EPS = 1e-5
HEADS, HD = 16, 16
GROUPS = 4
GH = HEADS // GROUPS
GW = GH * HD
NEG = -1e30


class Count:

    def __init__(self, sem, n, unroll=2, ahead=2):
        self.sem, self.n, self.unroll, self.ahead = sem, n, unroll, ahead

    def prime(self, eng):
        eng.sem_inc(self.sem, self.n * self.ahead)

    def of(self, i, u, k):
        return i * (self.unroll * self.n) + ((self.ahead + u) * self.n + k)

    def ago(self, i, u, d):
        return self.of(i, u, (1 - d) * self.n)


class Transfers:

    def __init__(self, even, odd, n):
        self.sems, self.n = (even, odd), 16 * n

    def prime(self, eng):
        for sem in self.sems:
            eng.sem_inc(sem, self.n)

    def done(self, i, u, k=None):
        return self.sems[u], i * self.n + (self.n + (self.n if k is None else 16 * k))

    def before(self, i, u):
        return self.sems[u], i * self.n + self.n


class Pool_:

    def __init__(self, nc, ctx, tag):
        self.nc, self.ctx, self.tag, self.sems = nc, ctx, tag, []
        ctx.callback(self.clear)

    def clear(self):
        self.nc.clear_and_free_semaphores(self.sems)
        self.nc.all_engine_barrier()

    def sb(self, name, shape, dt=F32):
        return self.ctx.enter_context(self.nc.sbuf_tensor(f"{self.tag}_{name}", shape, dt))

    def ps(self, name, shape, dt=F32):
        return self.ctx.enter_context(self.nc.psum_tensor(f"{self.tag}_{name}", shape, dt))

    def sem(self, name):
        self.sems.append(self.nc.alloc_semaphore(f"{self.tag}_{name}"))
        return self.sems[-1]

    def transfers(self, name, n=1):
        return Transfers(self.sem(name + "_even"), self.sem(name + "_odd"), n)

    def count(self, name, n, unroll=2, ahead=2):
        return Count(self.sem(name), n, unroll, ahead)


def skewed(eng, pairs, first, second):
    first(0, 0)
    with eng.Fori(0, pairs - 1) as i:
        first(i, 1)
        second(i, 0)
        first(i + 1, 0)
        second(i, 1)
    first(pairs - 1, 1)
    second(pairs - 1, 0)
    second(pairs - 1, 1)


def early(eng, pairs, first, second):
    first(0, 0)
    first(0, 1)
    with eng.Fori(0, pairs - 1) as i:
        for u in range(2):
            first(i + 1, u)
            second(i, u)
    second(pairs - 1, 0)
    second(pairs - 1, 1)


def start_of(eng, i, u, size, n=2):
    first = i * (n * size) + u * size
    return first if isinstance(i, int) else eng.snap(first)


def woven(eng, pairs, first, both, second):
    first(0, 0)
    with eng.Fori(0, pairs - 1) as i:
        both(i, 1, i, 0)
        both(i + 1, 0, i, 1)
    both(pairs - 1, 1, pairs - 1, 0)
    second(pairs - 1, 1)


class Gate:

    def __init__(self, sp, passed):
        self.sp, self.passed = sp, passed

    def wait_ge(self, sem, value):
        self.sp.wait_ge(sem, value)
        self.sp.sem_inc(self.passed, 1)




class Norm:

    def __init__(self, pool, ahead=2):
        self.stats = pool.sb("stats", [P, 2, CT, 6])
        self.mean_var = pool.sb("mean_var", [P, 2, CT, 2])
        self.std = pool.sb("std", [P, 2, CT])
        self.rstd = pool.sb("rstd", [P, 2, CT])
        self.eps = pool.sb("eps", [P, 1])
        self.var_ready = pool.count("var_ready", 1)
        self.std_ready = pool.count("std_ready", 1)
        self.eps_ready = pool.sem("eps_ready")

    def set_eps(self, nc, dve):
        nc.vector.memset(self.eps[:, :], EPS).then_inc(self.eps_ready, 1)

    def statistics(self, nc, dve, x, u):
        for t in range(CT):
            nc.vector.bn_stats(self.stats[:, u, t, :], x[:, t, :])
        dve.drain()
        for t in range(CT):
            last = nc.vector.bn_aggr(self.mean_var[:, u, t, :], self.stats[:, u, t, :])
        last.then_inc(self.var_ready.sem, 1)

    def deviation(self, nc, act, i, u):
        act.wait_ge(self.var_ready.sem, self.var_ready.of(i, u, 1))
        nc.scalar.activation(self.std[:, u, :], self.mean_var[:, u, :, 1], ACT.Sqrt,
                             bias=self.eps[:, 0:1]).then_inc(self.std_ready.sem, 1)

    def inverse(self, nc, dve, i, u):
        dve.wait_ge(self.std_ready.sem, self.std_ready.of(i, u, 1))
        nc.vector.reciprocal(self.rstd[:, u, :], self.std[:, u, :])
        dve.drain()

    def normalise(self, nc, out, x, u, t):
        return nc.vector.tensor_scalar(out, x, self.mean_var[:, u, t, 0:1], self.rstd[:, u, t:t + 1],
                                       ALU.subtract, ALU.mult)




def phase_qkv(nc, T):
    with ExitStack() as ctx:
        a = Pool_(nc, ctx, "A")
        ident = a.sb("ident", [P, P])
        w = a.sb("w", [P, KD, 3 * DIM])
        bias_qk = a.sb("bias_qk", [P, 4])
        bias_v = a.sb("bias_v", [P, DIM])
        x = a.sb("x", [P, 2, CT, DIM])
        xn = a.sb("xn", [P, 2, CT, DIM])
        xT = a.sb("xT", [P, 2, KD, CHUNK])
        qk = a.sb("qk", [P, 2, 4, CHUNK])
        rest = a.sb("rest", [P, 2, 4, CHUNK])
        parts = a.sb("parts", [P, 2, 3, 4, CHUNK], BF16)
        v = a.sb("v", [P, 2, CT, DIM])
        pT = a.ps("pT", [P, 2, KD, CHUNK])
        pO = a.ps("pO", [P, 4, CHUNK])
        norm = Norm(a)
        w_loaded = a.sem("w_loaded")
        x_loaded = a.transfers("x_loaded")
        xn_ready = a.count("xn_ready", 1)
        turned = a.count("turned", 1)
        xT_ready = a.count("xT_ready", 1)
        product = a.count("product", 6)
        qk_out = a.count("qk_out", 4)
        v_out = a.count("v_out", 2)
        part_ready = a.count("part_ready", 1)
        third_ready = a.count("third_ready", 1)
        qk_stored = a.transfers("qk_stored", 12)
        v_stored = a.transfers("v_stored", GROUPS)
        pairs = CHUNKS // 2
        block = ctx.enter_context(nc.Block())

        @block.sync
        def _(sp):
            x_loaded.prime(sp)
            qk_stored.prime(sp)
            v_stored.prime(sp)
            sp.dma_start(ident[:, :], T["ident"][:, :]).then_inc(w_loaded, 16)
            sp.dma_start(w[:, :, :], T["w_attn"].rearrange("(k p) n -> p k n", p=P)).then_inc(w_loaded, 16)
            sp.dma_start(bias_qk[:, :], T["b_attn"][0:2 * DIM].rearrange("(m p) -> p m", p=P)).then_inc(w_loaded, 16)
            sp.dma_start(bias_v[:, :], T["b_attn"][2 * DIM:3 * DIM].rearrange("(a n) -> a n", a=1)
                         .broadcast_to([P, DIM])).then_inc(w_loaded, 16)

            gate = Gate(sp, a.sem("passed"))

            def load(i, u):
                tok = start_of(sp, i, u, CHUNK)
                gate.wait_ge(xn_ready.sem, xn_ready.ago(i, u, 2))
                sp.dma_start(x[:, u, :, :], T["x"][bass.ds(tok, CHUNK), :].rearrange("(t p) d -> p t d", p=P)
                             ).then_inc(x_loaded.sems[u], 16)

            def store(i, u):
                seq = i if isinstance(i, int) else sp.snap(i * 1)
                gate.wait_ge(third_ready.sem, third_ready.of(i, u, 1))
                for part in range(3):
                    for m in range(4):
                        sp.dma_start(T[("q_parts", "k_parts")[m // 2]][
                            bass.ds(seq * DIM + part * SEQS * DIM + (m % 2) * P, P), u * CHUNK:(u + 1) * CHUNK],
                            parts[:, u, part, m, :]).then_inc(qk_stored.sems[u], 16)
                gate.wait_ge(v_out.sem, v_out.of(i, u, 2))
                for g in range(GROUPS):
                    sp.dma_start(T["v"][bass.ds(seq * (GROUPS * SEQ) + g * SEQ + u * CHUNK, CHUNK), :]
                                 .rearrange("(t p) d -> p t d", p=P), v[:, u, :, g * GW:(g + 1) * GW]
                                 ).then_inc(v_stored.sems[u], 16)

            early(sp, pairs, load, store)
            for u in range(2):
                gate.wait_ge(*qk_stored.done(pairs - 1, u))
                gate.wait_ge(*v_stored.done(pairs - 1, u))

        @block.vector
        def _(dve):
            xn_ready.prime(dve)
            norm.var_ready.prime(dve)
            v_out.prime(dve)
            norm.set_eps(nc, dve)
            dve.wait_ge(w_loaded, 64)

            def first(i, u):
                dve.wait_ge(*x_loaded.done(i, u))
                norm.statistics(nc, dve, x[:, u, :, :], u)
                norm.inverse(nc, dve, i, u)
                dve.wait_ge(turned.sem, turned.ago(i, u, 2))
                for t in range(CT):
                    last = norm.normalise(nc, xn[:, u, t, :], x[:, u, t, :], u, t)
                last.then_inc(xn_ready.sem, 1)

            def second(i, u):
                dve.wait_ge(*v_stored.before(i, u))
                for j in range(2):
                    dve.wait_ge(product.sem, product.of(i, u, 5 + j))
                    nc.vector.tensor_tensor(
                        v[:, u, 2 * j:2 * j + 2, :], pO[:, j, :].rearrange("p (t d) -> p t d", t=2),
                        bias_v[:, :].rearrange("p (a d) -> p a d", a=1).broadcast_to([P, 2, DIM]), ALU.add
                    ).then_inc(v_out.sem, 1)

            skewed(dve, pairs, first, second)

        @block.gpsimd
        def _(pool):
            third_ready.prime(pool)
            gate = Gate(pool, a.sem("pool_passed"))
            with pool.Fori(0, pairs) as i:
                for u in range(2):
                    gate.wait_ge(part_ready.sem, part_ready.of(i, u, 1))
                    nc.gpsimd.tensor_tensor(rest[:, u, :, :], qk[:, u, :, :], parts[:, u, 0, :, :], ALU.subtract)
                    pool.drain()
                    nc.gpsimd.tensor_copy(parts[:, u, 1, :, :], rest[:, u, :, :])
                    pool.drain()
                    nc.gpsimd.tensor_tensor(parts[:, u, 2, :, :], rest[:, u, :, :], parts[:, u, 1, :, :],
                                            ALU.subtract).then_inc(third_ready.sem, 1)

        @block.scalar
        def _(act):
            norm.std_ready.prime(act)
            xT_ready.prime(act)
            qk_out.prime(act)
            part_ready.prime(act)
            act.wait_ge(norm.eps_ready, 1)
            act.wait_ge(w_loaded, 64)

            def first(i, u):
                norm.deviation(nc, act, i, u)
                act.wait_ge(turned.sem, turned.of(i, u, 1))
                act.wait_ge(product.sem, product.ago(i, u, 2))
                nc.scalar.copy(xT[:, u, :, :], pT[:, u, :, :]).then_inc(xT_ready.sem, 1)

            def second(i, u):
                act.wait_ge(*qk_stored.before(i, u))
                act.wait_ge(third_ready.sem, third_ready.ago(i, u, 2))
                for m in range(4):
                    act.wait_ge(product.sem, product.of(i, u, m + 1))
                    nc.scalar.activation(qk[:, u, m, :], pO[:, m, :], ACT.Identity, bias=bias_qk[:, m:m + 1])
                    last = nc.scalar.activation(parts[:, u, 0, m, :], pO[:, m, :], ACT.Identity,
                                                bias=bias_qk[:, m:m + 1])
                    last.then_inc(qk_out.sem, 1)
                act.drain()
                act.sem_inc(part_ready.sem, 1)

            skewed(act, pairs, first, second)

        @block.tensor
        def _(pe):
            turned.prime(pe)
            product.prime(pe)
            pe.wait_ge(w_loaded, 64)

            def first(i, u):
                pe.wait_ge(xn_ready.sem, xn_ready.of(i, u, 1))
                pe.wait_ge(xT_ready.sem, xT_ready.ago(i, u, 2))
                for k in range(KD):
                    for t in range(CT):
                        last = nc.tensor.transpose(pT[:, u, k, t * P:(t + 1) * P], xn[:, u, t, k * P:(k + 1) * P],
                                                   ident[:, :])
                last.then_inc(turned.sem, 1)

            def second(i, u):
                pe.wait_ge(xT_ready.sem, xT_ready.of(i, u, 1))
                for m in range(4):
                    if m < 2:
                        pe.wait_ge(v_out.sem, v_out.of(i, u, m - 1))
                    else:
                        pe.wait_ge(qk_out.sem, qk_out.of(i, u, m - 3))
                    for k in range(KD):
                        last = nc.tensor.matmul(pO[:, m, :], w[:, k, m * P:(m + 1) * P], xT[:, u, k, :],
                                                start=k == 0, stop=k == KD - 1)
                    last.then_inc(product.sem, 1)
                for j in range(2):
                    pe.wait_ge(qk_out.sem, qk_out.of(i, u, j + 1))
                    for t in range(2):
                        for k in range(KD):
                            last = nc.tensor.matmul(pO[:, j, t * DIM:(t + 1) * DIM],
                                                    xT[:, u, k, (2 * j + t) * P:(2 * j + t + 1) * P],
                                                    w[:, k, 2 * DIM:3 * DIM], start=k == 0, stop=k == KD - 1)
                    last.then_inc(product.sem, 1)

            skewed(pe, pairs, first, second)





def attention_tables():
    slope = 0.5 ** np.arange(1, HEADS + 1)
    j = np.arange(SEQ)
    bf16 = mybir.dt.np(BF16)
    q_rows = np.zeros((4, GH, SEQ), bf16)
    q_rows[0] = q_rows[3] = 1.0
    k_rows = np.zeros((GROUPS, 4, GH, SEQ), np.float32)
    k_rows[:, 1:3] = 1.0
    k_rows[:, 0] = (4 * slope[:, None] * (j - j % 8)).reshape(GROUPS, GH, SEQ)
    k_rows[:, 3] = (4 * slope[:, None] * (j % 8)).reshape(GROUPS, GH, SEQ)
    middle = 512 * (np.arange(8) // 4) + 256
    centre = (4 * middle[:, None] * slope.reshape(GROUPS, 1, GH)).reshape(GROUPS, 1, 32)
    key = np.arange(P)[:, None] + 128 * (np.arange(8) - 4)[None] - 256
    key_bias = (key[None, :, :, None] * slope.reshape(GROUPS, 1, 1, GH)).reshape(GROUPS * P, 32)
    future = np.where(np.arange(P)[None] > np.arange(P)[:, None], NEG, 0.0).astype(np.float32)
    spread = np.zeros((P, P), np.float32)
    for h in range(GH):
        spread[32 * h + 16, 32 * h:32 * h + 32] = 1.0
    seqs = lambda t: np.ascontiguousarray(np.concatenate([t] * SEQS), np.float32)
    return {"q_rows": q_rows, "k_rows": seqs(k_rows.reshape(GROUPS * 4, GH, SEQ)).astype(bf16),
            "centre": seqs(centre.reshape(GROUPS, 32)),
            "key_bias": seqs(key_bias), "future": np.stack([future, future.T.copy()]), "spread": spread}


def phase_attention(nc, T):
    with ExitStack() as ctx:
        a = Pool_(nc, ctx, "B")
        QB = SEQ // P
        max_units = [(qb, kc, h) for qb in range(QB) for kc in range(1 + qb // 4) for h in range(GH)]
        exp_units = [(Q, kb, hp) for Q in range(2) for kb in range(4 * Q + 4) for hp in range(2)]
        NM, NE = len(max_units), len(exp_units)
        HALF = 8
        ident = a.sb("ident", [P, P])
        ident_b = a.sb("ident_b", [P, P], BF16)
        future = a.sb("future", [P, 2, P])
        future_b = a.sb("future_b", [P, 2, P], BF16)
        spread = a.sb("spread", [P, P])
        q = a.sb("q", [P, 2, GH, SEQ], BF16)
        k = a.sb("k", [P, 2, GH, SEQ], BF16)
        v_raw = a.sb("v_raw", [P, 2, QB, GW])
        v = a.sb("v", [P, 2, QB, GH, 32])
        centre = a.sb("centre", [P, 2, QB * GH])
        key_bias = a.sb("key_bias", [P, 2, 8, GH])
        part_max = a.sb("part_max", [P, 2, 2, QB, GH])
        row_max = a.sb("row_max", [P, QB * GH])
        minus_max = a.sb("minus_max", [P, QB, GH])
        shift = a.sb("shift", [P, 2, QB, P], BF16)
        probs = a.sb("probs", [P, 3, 2, 512])
        y = a.sb("y", [P, 2, 512])
        sums = a.sb("sums", [P, 2, 512])
        inv = a.sb("inv", [P, 2, 512])
        yn = a.sb("yn", [P, 2, 512])
        p_max = a.ps("p_max", [P, 2, 512])
        p_exp = a.ps("p_exp", [P, 2, 2, 512])
        p_acc = a.ps("p_acc", [P, 512])
        p_misc = a.ps("p_misc", [P, 512])
        fixed, FIXED = a.sem("fixed"), 16 * 3
        cast = a.sem("cast")
        cleared = a.sem("cleared")
        loaded = a.transfers("loaded", 17)
        v_ready = a.count("v_ready", 1)
        scored = a.count("scored", NM)
        maxed = a.count("maxed", NM)
        shift_ready = a.count("shift_ready", 1)
        shift_turned = a.count("shift_turned", 1)
        q_first = a.count("q_first", 1)
        q_second = a.count("q_second", 1)
        sum_spread = a.count("sum_spread", 2)
        sum_read = a.count("sum_read", 2)
        inv_ready = a.count("inv_ready", 2)
        scored_T = a.count("scored_T", NE)
        exped = a.count("exped", NE)
        weighted = a.count("weighted", NE)
        y_out = a.count("y_out", 2)
        yn_ready = a.count("yn_ready", 2)
        stored = [Count(a.sem(f"stored_{n}"), 64, 2, 1) for n in range(2)]
        pairs = SEQS * GROUPS // 2
        block = ctx.enter_context(nc.Block())

        LAG = 5

        def beside(n):
            at = lambda n: min(NM, max(0, n - LAG) * NM // (NE - 2 - LAG))
            return range(at(n), at(n + 1))

        def width(Q, kb):
            return max(0, kb - 4 * Q) * P

        @block.sync
        def _(sp):
            gate = Gate(sp, a.sem("passed"))
            loaded.prime(sp)
            stored[0].prime(sp)
            stored[1].prime(sp)
            for dst, src in ((ident[:, :], T["ident"][:, :]), (future[:, :, :], T["future"].rearrange("a p n -> p a n")),
                             (spread[:, :], T["spread"][:, :])):
                sp.dma_start(dst, src).then_inc(fixed, 16)

            sp.wait_ge(cleared, 1)

            def load(i, u):
                r64 = start_of(sp, i, u, GW)
                r4 = start_of(sp, i, u, 4)
                r1 = start_of(sp, i, u, 1)
                r128 = start_of(sp, i, u, P)
                r1024 = start_of(sp, i, u, SEQ)
                gate.wait_ge(weighted.sem, weighted.ago(i, u, 2))
                sem = loaded.sems[u]
                for n, (q_part, k_part) in enumerate(((0, 0), (0, 1), (1, 0), (1, 1), (0, 2), (2, 0))):
                    for x, name, part in ((q, "q_parts", q_part), (k, "k_parts", k_part)):
                        sp.dma_start(x[HD * n:HD * n + HD, u, :, :], T[name][bass.ds(r64 + part * SEQS * DIM, GW), :]
                                     .rearrange("(h d) t -> d h t", h=GH)).then_inc(sem, 16)
                sp.dma_start(k[96:100, u, :, :], T["k_rows"][bass.ds(r4, 4), :, :]).then_inc(sem, 16)
                sp.dma_start(q[96:100, u, :, :], T["q_rows"]).then_inc(sem, 16)
                sp.dma_start(v_raw[:, u, :, :], T["v"][bass.ds(r1024, SEQ), :].rearrange("(t p) d -> p t d", p=P)
                             ).then_inc(sem, 16)
                sp.dma_start(centre[:, u, :], T["centre"][bass.ds(r1, 1), :].broadcast_to([P, QB * GH])
                             ).then_inc(sem, 16)
                sp.dma_start(key_bias[:, u, :, :].rearrange("p a b -> p (a b)"), T["key_bias"][bass.ds(r128, P), :]
                             ).then_inc(sem, 16)

            def store(i, u):
                r64 = start_of(sp, i, u, GW)
                for Q in range(2):
                    gate.wait_ge(yn_ready.sem, yn_ready.of(i, u, Q + 1))
                    for h in range(GH):
                        sp.dma_start(T["yT"][bass.ds(r64 + HD * h, HD), 512 * Q:512 * Q + 512],
                                     yn[32 * h:32 * h + HD, Q, :]).then_inc(stored[Q].sem, 16)

            early(sp, pairs, load, store)
            for Q in range(2):
                sp.wait_ge(stored[Q].sem, stored[Q].of(pairs - 1, 1, 64))

        @block.gpsimd
        def _(pool):
            v_ready.prime(pool)
            yn_ready.prime(pool)
            for x in (q, k):
                nc.gpsimd.memset(x[96:P, :, :, :], 0.0)
                pool.drain()
            pool.sem_inc(cleared, 1)
            nc.gpsimd.memset(v[:, :, :, :, HD:32], 0.0)
            pool.drain()
            nc.gpsimd.memset(v[:, :, :, :, HD:HD + 1], 1.0)
            pool.drain()
            gate = Gate(pool, a.sem("pool_passed"))

            def values(i, u):
                gate.wait_ge(*loaded.done(i, u))
                nc.gpsimd.tensor_copy(v[:, u, :, :, 0:HD],
                                      v_raw[:, u, :, :].rearrange("p t (h d) -> p t h d", h=GH)
                                      ).then_inc(v_ready.sem, 1)
                pool.drain()

            def divide(i, u):
                for Q in range(2):
                    gate.wait_ge(inv_ready.sem, inv_ready.of(i, u, Q + 1))
                    gate.wait_ge(stored[Q].sem, stored[Q].ago(i, u, 1))
                    nc.gpsimd.tensor_tensor(yn[:, Q, :], y[:, Q, :], inv[:, Q, :], ALU.mult
                                            ).then_inc(yn_ready.sem, 1)
                    pool.drain()

            skewed(pool, pairs, values, divide)

        @block.vector
        def _(dve):
            maxed.prime(dve)
            shift_ready.prime(dve)
            q_first.prime(dve)
            sum_read.prime(dve)
            inv_ready.prime(dve)
            dve.wait_ge(fixed, FIXED)
            nc.vector.tensor_copy(ident_b[:, :], ident[:, :])
            nc.vector.memset(shift[:, :, :, :], 0.0)
            nc.vector.memset(part_max[:, :, 1, :, :], 4.0 * NEG)
            nc.vector.tensor_copy(future_b[:, :, :], future[:, :, :]).then_inc(cast, 1)
            dve.drain()

            def maxima(i, u, n):
                qb, kc, h = max_units[n]
                dve.wait_ge(scored.sem, scored.of(i, u, n + 1))
                keys = min(512, (qb + 1) * P - 512 * kc)
                nc.vector.reduce_max(part_max[:, u, kc, qb, h:h + 1], p_max[:, n % 2, 0:keys],
                                     AX.X).then_inc(maxed.sem, 1)

            def shifts(i, u):
                dve.drain()
                dve.wait_ge(*loaded.done(i, u))
                nc.vector.tensor_tensor(row_max[:, :], part_max[:, u, 0, :, :].rearrange("p a b -> p (a b)"),
                                        part_max[:, u, 1, :, :].rearrange("p a b -> p (a b)"), ALU.max)
                dve.drain()
                nc.vector.tensor_tensor(minus_max[:, :, :], centre[:, u, :].rearrange("p (a b) -> p a b", a=QB),
                                        row_max[:, :].rearrange("p (a b) -> p a b", a=QB), ALU.subtract)
                dve.drain()
                dve.wait_ge(shift_turned.sem, shift_turned.ago(i, u, 2))
                nc.vector.tensor_copy(shift[:, u, :, 1::32], minus_max[:, :, :])
                dve.drain()
                nc.vector.tensor_tensor(shift[:, u, :, 2::32], minus_max[:, :, :], shift[:, u, :, 1::32],
                                        ALU.subtract).then_inc(shift_ready.sem, 1)
                dve.wait_ge(shift_turned.sem, shift_turned.of(i, u, 1))
                for h in range(GH):
                    last = nc.vector.tensor_copy(q[96:P, u, h, 0:512], p_misc[32 * h:32 * h + 32, :])
                last.then_inc(q_first.sem, 1)

            def keep_sums(i, u, Q):
                dve.wait_ge(sum_spread.sem, sum_spread.of(i, u, Q + 1))
                dve.wait_ge(yn_ready.sem, yn_ready.of(i, u, Q - 1))
                nc.vector.tensor_copy(sums[:, Q, :], p_misc[:, :]).then_inc(sum_read.sem, 1)
                dve.drain()
                nc.vector.reciprocal(inv[:, Q, :], sums[:, Q, :]).then_inc(inv_ready.sem, 1)

            def first(i, u):
                for n in range(NM):
                    maxima(i, u, n)
                shifts(i, u)

            def both(i, u, j, w):
                for n in range(NE):
                    for m in beside(n):
                        maxima(i, u, m)
                    if n == HALF + 3:
                        keep_sums(j, w, 0)
                shifts(i, u)
                keep_sums(j, w, 1)

            def second(i, u):
                keep_sums(i, u, 0)
                keep_sums(i, u, 1)

            woven(dve, pairs, first, both, second)

        @block.scalar
        def _(act):
            exped.prime(act)
            y_out.prime(act)
            q_second.prime(act)

            def exps(i, u, n):
                Q, kb, hp = exp_units[n]
                skip = width(Q, kb)
                act.wait_ge(scored_T.sem, scored_T.of(i, u, n + 1))
                act.wait_ge(weighted.sem, weighted.of(i, u, n - 2))
                for e in range(2):
                    last = nc.scalar.activation(probs[:, n % 3, e, skip:512], p_exp[:, n % 2, e, skip:512], ACT.Exp,
                                                bias=key_bias[:, u, kb - 4 * Q + 4, 2 * hp + e:2 * hp + e + 1],
                                                scale=0.25)
                last.then_inc(exped.sem, 1)

            def take(i, u, Q):
                act.wait_ge(weighted.sem, weighted.of(i, u, (HALF, NE)[Q]))
                act.wait_ge(yn_ready.sem, yn_ready.of(i, u, Q - 1))
                nc.scalar.copy(y[:, Q, :], p_acc[:, :]).then_inc(y_out.sem, 1)

            def second(i, u):
                act.wait_ge(*loaded.done(i, u))
                act.wait_ge(shift_turned.sem, shift_turned.of(i, u, 1))
                for h in range(GH):
                    last = nc.scalar.copy(q[96:P, u, h, 512:SEQ], p_max[32 * h:32 * h + 32, 0, :])
                last.then_inc(q_second.sem, 1)
                for n in range(NE):
                    exps(i, u, n)
                    if n == HALF:
                        take(i, u, 0)
                take(i, u, 1)

            with act.Fori(0, pairs) as i:
                second(i, 0)
                second(i, 1)

        @block.tensor
        def _(pe):
            scored.prime(pe)
            shift_turned.prime(pe)
            sum_spread.prime(pe)
            scored_T.prime(pe)
            weighted.prime(pe)
            pe.wait_ge(cast, 1)
            pe.wait_ge(fixed, FIXED)

            def score(i, u, n):
                qb, kc, h = max_units[n]
                keys = min(512, (qb + 1) * P - 512 * kc)
                own = kc == qb // 4
                pe.wait_ge(maxed.sem, maxed.of(i, u, n - 1))
                last = nc.tensor.matmul(p_max[:, n % 2, 0:keys], q[:, u, h, qb * P:(qb + 1) * P],
                                        k[:, u, h, 512 * kc:512 * kc + keys], start=True, stop=not own)
                if own:
                    last = nc.tensor.matmul(p_max[:, n % 2, keys - P:keys], ident_b[:, :], future_b[:, 0, :],
                                            start=False, stop=True)
                last.then_inc(scored.sem, 1)

            def turn(i, u):
                pe.wait_ge(shift_ready.sem, shift_ready.of(i, u, 1))
                pe.wait_ge(sum_read.sem, sum_read.of(i, u, -1))
                for t in range(4):
                    nc.tensor.matmul(p_misc[:, t * P:(t + 1) * P], shift[:, u, t, :], ident_b[:, :],
                                     start=True, stop=True)
                for t in range(4):
                    last = nc.tensor.matmul(p_max[:, 0, t * P:(t + 1) * P], shift[:, u, 4 + t, :], ident_b[:, :],
                                            start=True, stop=True)
                last.then_inc(shift_turned.sem, 1)

            def score_T(i, u, n):
                Q, kb, hp = exp_units[n]
                skip = width(Q, kb)
                own = kb >= 4 * Q
                pe.wait_ge(exped.sem, exped.of(i, u, n - 1))
                if n == 0:
                    pe.wait_ge(q_first.sem, q_first.of(i, u, 1))
                if n == HALF:
                    pe.wait_ge(q_second.sem, q_second.of(i, u, 1))
                for e in range(2):
                    h = 2 * hp + e
                    last = nc.tensor.matmul(p_exp[:, n % 2, e, skip:512], k[:, u, h, kb * P:(kb + 1) * P],
                                            q[:, u, h, 512 * Q + skip:512 * Q + 512], start=True, stop=not own)
                if own:
                    for e in range(2):
                        last = nc.tensor.matmul(p_exp[:, n % 2, e, skip:skip + P], ident_b[:, :], future_b[:, 1, :],
                                                start=False, stop=True)
                last.then_inc(scored_T.sem, 1)

            def weigh(i, u, n):
                Q, kb, hp = exp_units[n]
                skip = width(Q, kb)
                if n == 0:
                    pe.wait_ge(v_ready.sem, v_ready.of(i, u, 1))
                if n == 0 or n == HALF:
                    pe.wait_ge(y_out.sem, y_out.of(i, u, n // HALF))
                pe.wait_ge(exped.sem, exped.of(i, u, n + 1))
                for e in range(2):
                    h = 2 * hp + e
                    last = nc.tensor.matmul(p_acc[32 * h:32 * h + 32, skip:512], v[:, u, kb, h, :],
                                            probs[:, n % 3, e, skip:512], start=kb == 0, stop=kb == 4 * Q + 3,
                                            tile_position=(0, 32 * h))
                last.then_inc(weighted.sem, 1)

            def spread_sum(i, u, Q):
                pe.wait_ge(y_out.sem, y_out.of(i, u, Q + 1))
                pe.wait_ge(sum_read.sem, sum_read.of(i, u, Q))
                nc.tensor.matmul(p_misc[:, :], spread[:, :], y[:, Q, :], start=True, stop=True
                                 ).then_inc(sum_spread.sem, 1)

            def exp_part(i, u, n):
                score_T(i, u, n)
                if n:
                    weigh(i, u, n - 1)
                if n == HALF + 2:
                    spread_sum(i, u, 0)

            def last_part(i, u):
                weigh(i, u, NE - 1)
                spread_sum(i, u, 1)

            def first(i, u):
                pe.wait_ge(*loaded.done(i, u))
                for n in range(NM):
                    score(i, u, n)
                turn(i, u)

            def both(i, u, j, w):
                for n in range(NE):
                    exp_part(j, w, n)
                    if n == LAG:
                        pe.wait_ge(*loaded.done(i, u))
                        pe.wait_ge(q_second.sem, q_second.of(j, w, 1))
                    for m in beside(n):
                        score(i, u, m)
                turn(i, u)
                pe.wait_ge(q_first.sem, q_first.of(i, u, 1))
                last_part(j, w)

            def second(i, u):
                for n in range(NE):
                    exp_part(i, u, n)
                last_part(i, u)

            woven(pe, pairs, first, both, second)




def phase_project(nc, T):
    with ExitStack() as ctx:
        a = Pool_(nc, ctx, "C")
        w = a.sb("w", [P, KD, DIM])
        bias = a.sb("bias", [P, CT, DIM])
        yT = a.sb("yT", [P, 2, KD, CHUNK])
        x = a.sb("x", [P, 2, CT, DIM])
        x1 = a.sb("x1", [P, 2, CT, DIM])
        z = a.sb("z", [P, 2, CT, DIM])
        out = a.ps("out", [P, 2, CT, DIM])
        norm = Norm(a)
        fixed = a.sem("fixed")
        loaded = a.transfers("loaded", 2)
        biased = a.count("biased", 1)
        product = a.count("product", 1)
        x1_ready = a.count("x1_ready", 1)
        z_ready = a.count("z_ready", 1)
        x1_stored = a.transfers("x1_stored")
        z_stored = a.transfers("z_stored")
        first_row = a.sem("first_row")
        pairs = CHUNKS // 2
        block = ctx.enter_context(nc.Block())

        @block.sync
        def _(sp):
            gate = Gate(sp, a.sem("passed"))
            for s in (loaded, x1_stored, z_stored):
                s.prime(sp)
            sp.dma_start(w[:, :, :], T["w_proj"].rearrange("(k p) n -> p k n", p=P)).then_inc(fixed, 16)
            for t in range(CT):
                sp.dma_start(bias[:, t, :], T["b_proj"].rearrange("(a n) -> a n", a=1).broadcast_to([P, DIM])
                             ).then_inc(fixed, 16)
            sp.dma_start(T["z"][0:1, :], T["zeros"][0:1, :]).then_inc(first_row, 16)

            def load(i, u):
                tok = start_of(sp, i, u, CHUNK)
                row = start_of(sp, i, 0, DIM, n=1)
                gate.wait_ge(product.sem, product.ago(i, u, 2))
                sp.dma_start(yT[:, u, :, :], T["yT"][bass.ds(row, DIM), u * CHUNK:(u + 1) * CHUNK]
                             .rearrange("(k p) n -> p k n", p=P)).then_inc(loaded.sems[u], 16)
                gate.wait_ge(x1_ready.sem, x1_ready.ago(i, u, 2))
                sp.dma_start(x[:, u, :, :], T["x"][bass.ds(tok, CHUNK), :].rearrange("(t p) d -> p t d", p=P)
                             ).then_inc(loaded.sems[u], 16)

            def store(i, u):
                tok = start_of(sp, i, u, CHUNK)
                gate.wait_ge(x1_ready.sem, x1_ready.of(i, u, 1))
                sp.dma_start(T["x1"][bass.ds(tok, CHUNK), :].rearrange("(t p) d -> p t d", p=P), x1[:, u, :, :]
                             ).then_inc(x1_stored.sems[u], 16)
                gate.wait_ge(z_ready.sem, z_ready.of(i, u, 1))
                sp.dma_start(T["z"][bass.ds(tok + 1, CHUNK), :].rearrange("(t p) d -> p t d", p=P), z[:, u, :, :]
                             ).then_inc(z_stored.sems[u], 16)

            early(sp, pairs, load, store)
            for u in range(2):
                sp.wait_ge(*x1_stored.done(pairs - 1, u))
                sp.wait_ge(*z_stored.done(pairs - 1, u))
            sp.wait_ge(first_row, 16)

        @block.gpsimd
        def _(pool):
            gate = Gate(pool, a.sem("pool_passed"))
            biased.prime(pool)
            pool.wait_ge(fixed, 16 * 5)
            with pool.Fori(0, pairs) as i:
                for u in range(2):
                    gate.wait_ge(*loaded.done(i, u))
                    nc.gpsimd.tensor_tensor(x[:, u, :, :], x[:, u, :, :], bias[:, :, :], ALU.add
                                            ).then_inc(biased.sem, 1)

        @block.vector
        def _(dve):
            for s in (x1_ready, z_ready, norm.var_ready):
                s.prime(dve)
            norm.set_eps(nc, dve)
            with dve.Fori(0, pairs) as i:
                for u in range(2):
                    dve.wait_ge(biased.sem, biased.of(i, u, 1))
                    dve.wait_ge(product.sem, product.of(i, u, 1))
                    dve.wait_ge(*x1_stored.before(i, u))
                    nc.vector.tensor_tensor(x1[:, u, :, :], out[:, u, :, :], x[:, u, :, :], ALU.add
                                            ).then_inc(x1_ready.sem, 1)
                    dve.drain()
                    norm.statistics(nc, dve, x1[:, u, :, :], u)
                    norm.inverse(nc, dve, i, u)
                    dve.wait_ge(*z_stored.before(i, u))
                    for t in range(CT):
                        last = norm.normalise(nc, z[:, u, t, :], x1[:, u, t, :], u, t)
                    last.then_inc(z_ready.sem, 1)

        @block.scalar
        def _(act):
            norm.std_ready.prime(act)
            act.wait_ge(norm.eps_ready, 1)
            with act.Fori(0, pairs) as i:
                for u in range(2):
                    norm.deviation(nc, act, i, u)

        @block.tensor
        def _(pe):
            product.prime(pe)
            pe.wait_ge(fixed, 16 * 5)
            with pe.Fori(0, pairs) as i:
                for u in range(2):
                    pe.wait_ge(*loaded.done(i, u))
                    pe.wait_ge(x1_ready.sem, x1_ready.ago(i, u, 2))
                    for t in range(CT):
                        for k in range(KD):
                            last = nc.tensor.matmul(out[:, u, t, :], yT[:, u, k, t * P:(t + 1) * P], w[:, k, :],
                                                    start=k == 0, stop=k == KD - 1)
                    last.then_inc(product.sem, 1)



LH, LD, WIN = 8, 64, 128
INNER = LH * LD
HALF_D = LD // 2


def rope_tables():
    half = np.arange(0, LD, 2).astype(np.float32)
    inv_freq = (np.float32(1.0) / (10000.0 ** (half.astype(np.float64) / LD)).astype(np.float32)).astype(np.float32)
    t = np.arange(SEQ, dtype=np.float32)
    freqs = (t[:, None] * inv_freq[None]).astype(np.float64)
    base = ((half + np.float32(0.4 * LD)) / np.float32(1.4 * LD)).astype(np.float64)
    scale = base[None] ** ((t[:, None] - SEQ // 2) / (WIN // 2))
    cos, sin = np.cos(freqs), np.sin(freqs)
    rows = [cos * scale, cos * scale, -sin * scale, sin * scale, cos / scale, cos / scale, -sin / scale, sin / scale]
    table = np.concatenate(rows, 1).astype(np.float32)
    own = np.where(np.arange(P)[None] > np.arange(P)[:, None], NEG, 0.0)
    before = np.where(np.arange(P)[None] < np.arange(P)[:, None], NEG, 0.0)
    flags = np.zeros((TILES // 2, P, 2), np.float32)
    flags[:, :, 0] = 1.0
    flags[::SEQ // P // 2, 0, 0] = 0.0
    flags[::SEQ // P // 2, :, 1] = NEG
    return {"rope": np.concatenate([table] * SEQS), "band": np.stack([own, before]).astype(np.float32),
            "flags": flags.reshape(-1, 2)}


def phase_window(nc, T, layer):
    with ExitStack() as ctx:
        a = Pool_(nc, ctx, f"D{layer}")
        ident = a.sb("ident", [P, P])
        ident_b = a.sb("ident_b", [P, P], BF16)
        band = a.sb("band", [P, 2, P])
        mask = a.sb("mask", [P, 2, 2, P], BF16)
        wqkv = a.sb("wqkv", [P, KD, 3 * INNER])
        wo = a.sb("wo", [P, INNER // P, DIM])
        factor = a.sb("factor", [P, 4, LD])
        power = a.sb("power", [P, 2 * LH])
        h = a.sb("h", [P, 2, DIM])
        rest = a.sb("rest", [P, 2, P])
        rope = a.sb("rope", [P, 2, 4, LD])
        flags = a.sb("flags", [P, 2, 2])
        hT = a.sb("hT", [P, 2, KD, P])
        square = a.sb("square", [P, 2 * LH, LD])
        norm2 = a.sb("norm2", [P, 2 * LH])
        rnorm = a.sb("rnorm", [P, 2, 2 * LH])
        rq = a.sb("rq", [P, 2, LH])
        kn = a.sb("kn", [P, LH, LD])
        qa = a.sb("qa", [P, LH, LD])
        qb = a.sb("qb", [P, LH, LD])
        ka = a.sb("ka", [P, LH, LD])
        kb = a.sb("kb", [P, LH, LD])
        qr = a.sb("qr", [P, LH, LD])
        kr = a.sb("kr", [P, LH, LD])
        qT = a.sb("qT", [P, 2, LH // 2, P])
        kT = a.sb("kT", [P, LH // 2, 2, P])
        v = a.sb("v", [P, 2, INNER])
        top = a.sb("top", [P, LH])
        neg = a.sb("neg", [P, LH])
        total = a.sb("total", [P, LH])
        inv = a.sb("inv", [P, LH])
        probs = a.sb("probs", [P, LH, 2, P])
        pT = a.sb("pT", [P, LH, 2, P])
        y = a.sb("y", [P, LH, LD])
        yT = a.sb("yT", [P, INNER // P, P])
        z1 = a.sb("z1", [P, 2, DIM])
        first_half = a.sb("first_half", [P, 2, P])
        scores = a.ps("scores", [P, LH, 2, P])
        front = a.ps("front", [P, 4, 512])
        p_y = scores[:, 0:2, :, :].rearrange("p a b c -> p (a b c)")
        p_yT = scores[:, 2:4, :, :].rearrange("p a b c -> p (a b c)")
        p_z = scores[:, 4:5, :, :].rearrange("p a b c -> p (a b c)")
        fixed = a.sem("fixed")
        cast = a.sem("cast")
        loaded = a.transfers("loaded", 4)
        rest_loaded = a.transfers("rest_loaded")
        h_ready = a.count("h_ready", 1)
        h_turned = a.count("h_turned", 1)
        hT_ready = a.count("hT_ready", 1)
        qkv = a.count("qkv", 3)
        squared = a.count("squared", 2)
        norm_ready = a.count("norm_ready", 1)
        inverse_ready = a.count("inverse_ready", 1)
        qab_ready = a.count("qab_ready", 1)
        q_rotated = a.count("q_rotated", 1)
        k_rotated = a.count("k_rotated", 1)
        qk_turned = a.count("qk_turned", 2)
        qkT_ready = a.count("qkT_ready", 2)
        v_ready = a.count("v_ready", 1)
        scored = a.count("scored", 2)
        neg_ready = a.count("neg_ready", 1)
        exped = a.count("exped", 2)
        p_turned = a.count("p_turned", 2)
        pT_ready = a.count("pT_ready", 1)
        pT_ready_2 = a.count("pT_ready_2", 1)
        weighted = a.count("weighted", 1)
        y_ready = a.count("y_ready", 1)
        y_turned = a.count("y_turned", 1)
        yT_ready = a.count("yT_ready", 1)
        projected = a.count("projected", 1)
        z1_ready = a.count("z1_ready", 1)
        stored = a.transfers("stored")
        first_row = a.sem("first_row")
        pairs = TILES // 2
        NFIX = 14
        block = ctx.enter_context(nc.Block())

        @block.sync
        def _(sp):
            gate = Gate(sp, a.sem("passed"))
            for s in (loaded, rest_loaded, stored):
                s.prime(sp)
            sp.dma_start(T["z1"][0:1, :], T["zeros"][0:1, :]).then_inc(first_row, 16)
            sp.dma_start(ident[:, :], T["ident"][:, :]).then_inc(fixed, 16)
            sp.dma_start(band[:, :, :], T["band"].rearrange("a p n -> p a n")).then_inc(fixed, 16)
            sp.dma_start(wqkv[:, :, :], T["wqkv"][layer].rearrange("(k p) n -> p k n", p=P)).then_inc(fixed, 16)
            sp.dma_start(wo[:, :, :], T["wo"][layer].rearrange("(k p) n -> p k n", p=P)).then_inc(fixed, 16)
            for n, name in enumerate(("q_scale", "k_scale")):
                row = T[name][layer:layer + 1, :]
                sp.dma_start(factor[:, 2 * n, :], row.broadcast_to([P, LD])).then_inc(fixed, 16)
                for side in range(2):
                    here, other = side * HALF_D, (1 - side) * HALF_D
                    sp.dma_start(factor[:, 2 * n + 1, here:here + HALF_D],
                                 row[:, other:other + HALF_D].broadcast_to([P, HALF_D])).then_inc(fixed, 16)

            def load(i, u):
                tok = start_of(sp, i, u, P)
                i128 = start_of(sp, i, 0, P, n=1)
                gate.wait_ge(q_rotated.sem, q_rotated.ago(i, u, 2))
                gate.wait_ge(k_rotated.sem, k_rotated.ago(i, u, 2))
                sem = loaded.sems[u]
                sp.dma_start(h[:, u, 0:P], T["z"][bass.ds(tok + 1, P), 0:P]).then_inc(sem, 16)
                sp.dma_start(h[:, u, P:DIM], T["z"][bass.ds(tok, P), P:DIM]).then_inc(sem, 16)
                sp.dma_start(rope[:, u, :, :], T["rope"][bass.ds(tok, P), :].rearrange("p (a d) -> p a d", a=4)
                             ).then_inc(sem, 16)
                sp.dma_start(flags[:, u, :], T["flags"][bass.ds(i128, P), :]).then_inc(sem, 16)
                gate.wait_ge(z1_ready.sem, z1_ready.ago(i, u, 2))
                sp.dma_start(rest[:, u, :], T["z"][bass.ds(tok + 1, P), P:DIM]).then_inc(rest_loaded.sems[u], 16)

            def store(i, u):
                tok = start_of(sp, i, u, P)
                gate.wait_ge(z1_ready.sem, z1_ready.of(i, u, 1))
                sp.dma_start(T["z1"][bass.ds(tok + 1, P), :], z1[:, u, :]).then_inc(stored.sems[u], 16)

            early(sp, pairs, load, store)
            for u in range(2):
                sp.wait_ge(*stored.done(pairs - 1, u))
            sp.wait_ge(first_row, 16)

        place = [n ^ 3 if n % 4 in (1, 2) else n for n in range(LH)]

        def quarters(eng, front0, front1, back1, front2, back2, back3):
            front0(0, 0)
            front1(0, 0)
            front2(0, 0)
            front0(0, 1)
            with eng.Fori(0, pairs - 1) as i:
                for at, before, after in (((i, 1), (i, 0), (i + 1, 0)), ((i + 1, 0), (i, 1), (i + 1, 1))):
                    front1(*at)
                    back1(*before)
                    front2(*at)
                    back2(*before)
                    front0(*after)
                    back3(*before)
            last = pairs - 1
            front1(last, 1)
            back1(last, 0)
            front2(last, 1)
            back2(last, 0)
            back3(last, 0)
            back1(last, 1)
            back2(last, 1)
            back3(last, 1)

        def nothing(i, u):
            pass

        @block.gpsimd
        def _(pool):
            gate = Gate(pool, a.sem("pool_passed"))
            for s in (h_ready, inverse_ready, q_rotated):
                s.prime(pool)
            nc.gpsimd.memset(power[:, :], -0.5)
            nc.gpsimd.memset(kT[:, :, 1, :], 0.0)
            nc.gpsimd.memset(v[:, 1, :], 0.0)
            pool.wait_ge(fixed, 16 * 10)
            pool.drain()
            nc.gpsimd.tensor_copy(ident_b[:, :], ident[:, :])
            nc.gpsimd.tensor_copy(mask[:, 0, 0, :], band[:, 0, :])
            nc.gpsimd.tensor_copy(mask[:, 1, 1, :], band[:, 0, :])
            nc.gpsimd.tensor_copy(mask[:, 1, 0, :], band[:, 1, :])
            pool.drain().then_inc(cast, 1)

            def step(i, u):
                gate.wait_ge(*loaded.done(i, u))
                if u == 0:
                    gate.wait_ge(scored.sem, scored.ago(i, u, 2))
                    nc.gpsimd.tensor_scalar(mask[:, 0, 1, :], band[:, 1, :], flags[:, u, 1:2], None, ALU.add)
                    nc.gpsimd.tensor_scalar(h[:, u, P:DIM], h[:, u, P:DIM], flags[:, u, 0:1], None, ALU.mult)
                nc.gpsimd.tensor_tensor(rope[:, u, :, :], rope[:, u, :, :], factor[:, :, :], ALU.mult)
                pool.drain().then_inc(h_ready.sem, 1)
                gate.wait_ge(norm_ready.sem, norm_ready.of(i, u, 1))
                nc.gpsimd.tensor_tensor(rnorm[:, u, :], norm2[:, :], power[:, :], ALU.pow)
                pool.drain()
                nc.gpsimd.tensor_scalar(rnorm[:, u, :], rnorm[:, u, :], 1e12, None, ALU.min
                                        ).then_inc(inverse_ready.sem, 1)
                pool.drain()
                gate.wait_ge(qab_ready.sem, qab_ready.of(i, u, 1))
                gate.wait_ge(qk_turned.sem, qk_turned.ago(i, u, 1))
                nc.gpsimd.tensor_tensor(qr[:, :, :], qa[:, :, :], qb[:, :, :], ALU.add).then_inc(q_rotated.sem, 1)
                pool.drain()

            with pool.Fori(0, pairs) as i:
                step(i, 0)
                step(i, 1)

        @block.vector
        def _(dve):
            for s in (norm_ready, k_rotated, qab_ready, neg_ready, pT_ready, y_ready, z1_ready):
                s.prime(dve)

            def front1(i, u):
                lo, hi = slice(0, HALF_D), slice(HALF_D, LD)
                q = front[:, 1, :].rearrange("p (h d) -> p h d", h=LH)
                bc = lambda n, s: rope[:, u, n:n + 1, s].broadcast_to([P, LH, s.stop - s.start])
                dve.wait_ge(squared.sem, squared.of(i, u, 1))
                dve.wait_ge(inverse_ready.sem, inverse_ready.ago(i, u, 1))
                nc.vector.tensor_reduce(norm2[:, 0:LH], square[:, 0:LH, :], AX.X, ALU.add)
                dve.wait_ge(h_ready.sem, h_ready.of(i, u, 1))
                dve.wait_ge(q_rotated.sem, q_rotated.ago(i, u, 1))
                nc.vector.tensor_tensor(qa[:, :, :], q, bc(0, slice(0, LD)), ALU.mult)
                nc.vector.tensor_tensor(qb[:, :, lo], q[:, :, hi], bc(1, lo), ALU.mult)
                nc.vector.tensor_tensor(qb[:, :, hi], q[:, :, lo], bc(1, hi), ALU.mult).then_inc(qab_ready.sem, 1)
                dve.wait_ge(squared.sem, squared.of(i, u, 2))
                nc.vector.tensor_reduce(norm2[:, LH:2 * LH], square[:, LH:2 * LH, :], AX.X, ALU.add
                                        ).then_inc(norm_ready.sem, 1)

            def back1(i, u):
                for n in range(2):
                    dve.wait_ge(scored.sem, scored.of(i, u, n + 1))
                    nc.vector.tensor_reduce(top[:, 4 * n:4 * n + 4].rearrange("p (b a) -> p a b", b=2),
                                            scores[:, 4 * n:4 * n + 4, :, :]
                                            .rearrange("p (a b) s k -> p a b (s k)", a=2), AX.X, ALU.max)
                dve.drain()
                dve.wait_ge(exped.sem, exped.ago(i, u, 1))
                nc.vector.scalar_tensor_tensor(neg[:, :], top[:, :], -1.0, rq[:, u, :], ALU.mult, ALU.mult
                                               ).then_inc(neg_ready.sem, 1)

            def front2(i, u):
                lo, hi = slice(0, HALF_D), slice(HALF_D, LD)
                k = front[:, 2, :].rearrange("p (h d) -> p h d", h=LH)
                bc = lambda n, s: rope[:, u, n:n + 1, s].broadcast_to([P, LH, s.stop - s.start])
                dve.wait_ge(inverse_ready.sem, inverse_ready.of(i, u, 1))
                dve.wait_ge(exped.sem, exped.ago(i, u, 2))
                nc.vector.tensor_scalar(rq[:, u, :], rnorm[:, u, 0:LH], 8.0, None, ALU.mult)
                nc.vector.tensor_tensor(kn[:, :, :], k, rnorm[:, u, LH:2 * LH].rearrange("p (h a) -> p h a", a=1)
                                        .broadcast_to([P, LH, LD]), ALU.mult)
                dve.drain()
                nc.vector.tensor_tensor(ka[:, :, :], kn[:, :, :], bc(2, slice(0, LD)), ALU.mult)
                nc.vector.tensor_tensor(kb[:, :, lo], kn[:, :, hi], bc(3, lo), ALU.mult)
                nc.vector.tensor_tensor(kb[:, :, hi], kn[:, :, lo], bc(3, hi), ALU.mult)
                dve.drain()
                dve.wait_ge(qk_turned.sem, qk_turned.ago(i, u, 1))
                nc.vector.tensor_tensor(kr[:, :, :], ka[:, :, :], kb[:, :, :], ALU.add).then_inc(k_rotated.sem, 1)

            def back2(i, u):
                dve.wait_ge(exped.sem, exped.of(i, u, 2))
                nc.vector.reciprocal(inv[:, :], total[:, :])
                dve.wait_ge(p_turned.sem, p_turned.of(i, u, 1))
                dve.wait_ge(weighted.sem, weighted.ago(i, u, 1))
                nc.vector.tensor_copy(pT[:, 0:4, :, :], scores[:, 0:4, :, :]).then_inc(pT_ready.sem, 1)
                dve.wait_ge(weighted.sem, weighted.of(i, u, 1))
                nc.vector.tensor_tensor(y[:, :, :], p_y.rearrange("p (h d) -> p h d", h=LH),
                                        inv[:, :].rearrange("p (h a) -> p h a", a=1).broadcast_to([P, LH, LD]),
                                        ALU.mult).then_inc(y_ready.sem, 1)
                dve.wait_ge(projected.sem, projected.of(i, u, 1))
                dve.wait_ge(*rest_loaded.done(i, u))
                dve.wait_ge(*stored.before(i, u))
                nc.vector.tensor_tensor(z1[:, u, 0:P], p_z[:, 0:P], first_half[:, u, :], ALU.add)
                nc.vector.tensor_tensor(z1[:, u, P:DIM], p_z[:, P:DIM], rest[:, u, :], ALU.add
                                        ).then_inc(z1_ready.sem, 1)

            quarters(dve, nothing, front1, back1, front2, back2, nothing)

        @block.scalar
        def _(act):
            for s in (hT_ready, squared, qkT_ready, v_ready, exped, pT_ready_2, yT_ready):
                s.prime(act)

            def front0(i, u):
                act.wait_ge(h_turned.sem, h_turned.of(i, u, 1))
                act.wait_ge(qkv.sem, qkv.ago(i, u, 2))
                nc.scalar.copy(hT[:, u, :, :].rearrange("p k n -> p (k n)"), front[:, 0, 0:KD * P]
                               ).then_inc(hT_ready.sem, 1)

            def front1(i, u):
                act.wait_ge(z1_ready.sem, z1_ready.ago(i, u, 2))
                nc.scalar.copy(first_half[:, u, :], h[:, u, 0:P])
                act.wait_ge(norm_ready.sem, norm_ready.ago(i, u, 1))
                for n in range(2):
                    act.wait_ge(qkv.sem, qkv.of(i, u, n + 1))
                    nc.scalar.activation(square[:, n * LH:(n + 1) * LH, :].rearrange("p h d -> p (h d)"),
                                         front[:, 1 + n, :], ACT.Square).then_inc(squared.sem, 1)

            def back1(i, u):
                act.wait_ge(qkv.sem, qkv.of(i, u, 3))
                act.wait_ge(weighted.sem, weighted.ago(i, u, 1))
                nc.scalar.copy(v[:, u, :], front[:, 3, :]).then_inc(v_ready.sem, 1)
                act.wait_ge(neg_ready.sem, neg_ready.of(i, u, 1))
                act.wait_ge(p_turned.sem, p_turned.ago(i, u, 1))
                act.wait_ge(y_ready.sem, y_ready.ago(i, u, 1))
                for n in range(LH):
                    last = nc.scalar.activation(probs[:, place[n], :, :].rearrange("p a b -> p (a b)"),
                                                scores[:, place[n], :, :].rearrange("p a b -> p (a b)"), ACT.Exp,
                                                bias=neg[:, n:n + 1], scale=rq[:, u, n:n + 1],
                                                accum_out=total[:, n:n + 1])
                    if n % 4 == 3:
                        last.then_inc(exped.sem, 1)

            def front2(i, u):
                for n, (dst, bank) in enumerate(((qT[:, u, :, :], 1), (kT[:, :, u, :], 2))):
                    act.wait_ge(qk_turned.sem, qk_turned.of(i, u, n + 1))
                    act.wait_ge(scored.sem, scored.ago(i, u, 1))
                    nc.scalar.copy(dst, front[:, bank, :].rearrange("p (a b) -> p a b", b=P)
                                   ).then_inc(qkT_ready.sem, 1)

            def back2(i, u):
                act.wait_ge(p_turned.sem, p_turned.of(i, u, 2))
                nc.scalar.copy(pT[:, 4:8, :, :].rearrange("p a b c -> p (a b c)"),
                               scores[:, 4:8, :, :].rearrange("p a b c -> p (a b c)")).then_inc(pT_ready_2.sem, 1)

            def back3(i, u):
                act.wait_ge(y_turned.sem, y_turned.of(i, u, 1))
                act.wait_ge(projected.sem, projected.ago(i, u, 1))
                nc.scalar.copy(yT[:, :, :].rearrange("p k n -> p (k n)"), p_yT).then_inc(yT_ready.sem, 1)

            quarters(act, front0, front1, back1, front2, back2, back3)

        @block.tensor
        def _(pe):
            for s in (h_turned, qkv, qk_turned, scored, p_turned, weighted, y_turned, projected):
                s.prime(pe)
            pe.wait_ge(fixed, 16 * 10)
            pe.wait_ge(cast, 1)

            def front0(i, u):
                pe.wait_ge(h_ready.sem, h_ready.of(i, u, 1))
                pe.wait_ge(hT_ready.sem, hT_ready.ago(i, u, 1))
                for k in range(KD):
                    last = nc.tensor.transpose(front[:, 0, k * P:(k + 1) * P], h[:, u, k * P:(k + 1) * P], ident[:, :])
                last.then_inc(h_turned.sem, 1)

            def project(i, u, products):
                for m in products:
                    if m < 2:
                        pe.wait_ge(qkT_ready.sem, qkT_ready.ago(i, u, 1))
                    else:
                        pe.wait_ge(v_ready.sem, v_ready.ago(i, u, 1))
                    for k in range(KD):
                        last = nc.tensor.matmul(front[:, 1 + m, :], hT[:, u, k, :],
                                                wqkv[:, k, m * INNER:(m + 1) * INNER], start=k == 0, stop=k == KD - 1)
                    last.then_inc(qkv.sem, 1)

            def front1(i, u):
                pe.wait_ge(hT_ready.sem, hT_ready.of(i, u, 1))
                project(i, u, (0, 1))

            def front2(i, u):
                project(i, u, (2,))
                pe.wait_ge(k_rotated.sem, k_rotated.of(i, u, 1))
                pe.wait_ge(q_rotated.sem, q_rotated.of(i, u, 1))
                for n, src in enumerate((qr, kr)):
                    for t in range(LH // 2):
                        last = nc.tensor.transpose(front[:, 1 + n, t * P:(t + 1) * P],
                                                   src[:, 2 * t:2 * t + 2, :].rearrange("p a b -> p (a b)"), ident[:, :])
                    last.then_inc(qk_turned.sem, 1)

            def back1(i, u):
                pe.wait_ge(qkT_ready.sem, qkT_ready.of(i, u, 2))
                pe.wait_ge(z1_ready.sem, z1_ready.ago(i, u, 1))
                for n in range(2):
                    for bank in range(4 * n, 4 * n + 4, 2):
                        nc.tensor.matmul(scores[:, bank:bank + 2, :, :].rearrange("p h a b -> p h (a b)"), ident_b[:, :],
                                         mask[:, u:u + 1, :, :].rearrange("p h a b -> p h (a b)")
                                         .broadcast_to([P, 2, 2 * P]), start=True, stop=False)
                    for m in range(4 * n, 4 * n + 4):
                        strip = slice(LD * (m % 2), LD * (m % 2) + LD)
                        last = nc.tensor.matmul(scores[:, place[m], :, :].rearrange("p a b -> p (a b)"),
                                                qT[strip, u, m // 2, :],
                                                kT[strip, m // 2, :, :].rearrange("p a b -> p (a b)"),
                                                start=False, stop=m % 4 >= 2)
                    last.then_inc(scored.sem, 1)

            def back2(i, u):
                for n in range(2):
                    pe.wait_ge(exped.sem, exped.of(i, u, n + 1))
                    for m in range(4 * n, 4 * n + 4):
                        for s in range(2):
                            last = nc.tensor.transpose(scores[:, m, s, :], probs[:, m, s, :], ident[:, :])
                    last.then_inc(p_turned.sem, 1)
                pe.wait_ge(pT_ready.sem, pT_ready.of(i, u, 1))
                pe.wait_ge(pT_ready_2.sem, pT_ready_2.of(i, u, 1))
                pe.wait_ge(v_ready.sem, v_ready.of(i, u, 1))
                for n in range(LH):
                    for s in range(2):
                        last = nc.tensor.matmul(p_y[:, n * LD:(n + 1) * LD], pT[:, place[n], s, :],
                                                v[:, s, n * LD:(n + 1) * LD], start=s == 0, stop=s == 1)
                last.then_inc(weighted.sem, 1)

            def back3(i, u):
                pe.wait_ge(y_ready.sem, y_ready.of(i, u, 1))
                for k in range(INNER // P):
                    last = nc.tensor.transpose(p_yT[:, k * P:(k + 1) * P],
                                               y[:, 2 * k:2 * k + 2, :].rearrange("p a b -> p (a b)"), ident[:, :])
                last.then_inc(y_turned.sem, 1)
                pe.wait_ge(yT_ready.sem, yT_ready.of(i, u, 1))
                for k in range(INNER // P):
                    last = nc.tensor.matmul(p_z[:, :], yT[:, k, :], wo[:, k, :], start=k == 0,
                                            stop=k == INNER // P - 1)
                last.then_inc(projected.sem, 1)

            quarters(pe, front0, front1, back1, front2, back2, back3)



HID = int(DIM * 4 * 2 / 3)
FM = -(-HID // P)
FW = [min(P, HID - m * P) for m in range(FM)]


def phase_feed_forward(nc, T, layer, last_layer):
    with ExitStack() as ctx:
        a = Pool_(nc, ctx, f"E{layer}")
        src, dst = T["z1"], T["x2"] if last_layer else T["z"]
        ident = a.sb("ident", [P, P])
        w1 = a.sb("w1", [P, KD, 2 * HID])
        w2 = a.sb("w2", [P, FM, DIM])
        gain = a.sb("gain", [P, KD])
        shift = a.sb("shift", [P, KD])
        b1 = a.sb("b1", [P, 2, FM])
        b2 = a.sb("b2", [P, CT, DIM])
        keep = a.sb("keep", [P, 1])
        h = a.sb("h", [P, 2, CT, DIM])
        rest = a.sb("rest", [P, 2, CT, DIM])
        x1 = a.sb("x1", [P, 2, CT, DIM])
        hn = a.sb("hn", [P, 2, CT, DIM])
        hT = a.sb("hT", [P, 2, KD, CHUNK])
        gated = a.sb("gated", [P, 2, CHUNK])
        act_out = a.sb("act_out", [P, 2, FM, CHUNK])
        z2 = a.sb("z2", [P, 2, CT, DIM])
        p_T = a.ps("p_T", [P, KD, CHUNK])
        p_ag = a.ps("p_ag", [P, 2, 2, CHUNK])
        p_out = a.ps("p_out", [P, CT, DIM])
        norm = Norm(a)
        fixed = a.sem("fixed")
        loaded = a.transfers("loaded", 2)
        rest_loaded = a.transfers("rest_loaded", 2 if last_layer else 1)
        rest_ready = a.count("rest_ready", 1)
        hn_ready = a.count("hn_ready", 1)
        turned = a.count("turned", 1)
        hT_ready = a.count("hT_ready", 1)
        product = a.count("product", FM)
        gelu = a.count("gelu", FM)
        act_ready = a.count("act_ready", FM)
        summed = a.count("summed", 1)
        z2_ready = a.count("z2_ready", 1)
        stored = a.transfers("stored")
        pairs = CHUNKS // 2
        NFIX = 9 + CT
        off = 0 if last_layer else 1
        block = ctx.enter_context(nc.Block())

        @block.sync
        def _(sp):
            gate = Gate(sp, a.sem("passed"))
            for s in (loaded, rest_loaded, stored):
                s.prime(sp)
            full = (FM - 1) * P
            col = lambda ap: ap.rearrange("(m p) -> p m", p=P)
            one = lambda ap: ap.rearrange("(p m) -> p m", m=1)
            for out_, in_ in (
                (ident[:, :], T["ident"][:, :]),
                (w1[:, :, :], T["w1"][layer].rearrange("(k p) n -> p k n", p=P)),
                (w2[:, 0:FM - 1, :], T["w2"][layer, 0:full, :].rearrange("(m p) n -> p m n", p=P)),
                (w2[0:FW[-1], FM - 1, :], T["w2"][layer, full:HID, :]),
                (gain[:, :], col(T["ln_g"][layer])),
                (shift[:, :], col(T["ln_b"][layer])),
                (keep[:, :], T["flags"][0:P, 0:1]),
            ):
                sp.dma_start(out_, in_).then_inc(fixed, 16)
            for n in range(2):
                sp.dma_start(b1[:, n, 0:FM - 1], col(T["b1"][layer, n * HID:n * HID + full])).then_inc(fixed, 16)
                sp.dma_start(b1[0:FW[-1], n, FM - 1:FM], one(T["b1"][layer, n * HID + full:(n + 1) * HID])
                             ).then_inc(fixed, 16)
            for t in range(CT):
                sp.dma_start(b2[:, t, :], T["b2"][layer:layer + 1, :].broadcast_to([P, DIM])).then_inc(fixed, 16)

            def load(i, u):
                tok = start_of(sp, i, u, CHUNK)
                gate.wait_ge(hn_ready.sem, hn_ready.ago(i, u, 2))
                tiles = lambda ap: ap.rearrange("(t p) d -> p t d", p=P)
                sp.dma_start(h[:, u, :, 0:P], tiles(src[bass.ds(tok + 1, CHUNK), 0:P])).then_inc(loaded.sems[u], 16)
                sp.dma_start(h[:, u, :, P:DIM], tiles(src[bass.ds(tok, CHUNK), P:DIM])).then_inc(loaded.sems[u], 16)
                gate.wait_ge(z2_ready.sem, z2_ready.ago(i, u, 2))
                sp.dma_start(rest[:, u, :, :], tiles(src[bass.ds(tok + 1, CHUNK), :])).then_inc(rest_loaded.sems[u], 16)
                if last_layer:
                    sp.dma_start(x1[:, u, :, :], tiles(T["x1"][bass.ds(tok, CHUNK), :])
                                 ).then_inc(rest_loaded.sems[u], 16)

            def store(i, u):
                tok = start_of(sp, i, u, CHUNK)
                gate.wait_ge(z2_ready.sem, z2_ready.of(i, u, 1))
                sp.dma_start(dst[bass.ds(tok + off, CHUNK), :].rearrange("(t p) d -> p t d", p=P), z2[:, u, :, :]
                             ).then_inc(stored.sems[u], 16)

            early(sp, pairs, load, store)
            for u in range(2):
                sp.wait_ge(*stored.done(pairs - 1, u))

        @block.gpsimd
        def _(pool):
            gate = Gate(pool, a.sem("pool_passed"))
            rest_ready.prime(pool)
            pool.wait_ge(fixed, 16 * (11 + CT))
            with pool.Fori(0, pairs) as i:
                for u in range(2):
                    gate.wait_ge(*rest_loaded.done(i, u))
                    nc.gpsimd.tensor_tensor(rest[:, u, :, :], rest[:, u, :, :], b2[:, :, :], ALU.add)
                    pool.drain()
                    if last_layer:
                        nc.gpsimd.tensor_tensor(rest[:, u, :, :], rest[:, u, :, :], x1[:, u, :, :], ALU.add)
                        pool.drain()
                    pool.sem_inc(rest_ready.sem, 1)

        @block.vector
        def _(dve):
            for s in (norm.var_ready, hn_ready, act_ready, z2_ready):
                s.prime(dve)
            norm.set_eps(nc, dve)
            dve.wait_ge(fixed, 16 * (11 + CT))

            def first(i, u):
                dve.wait_ge(*loaded.done(i, u))
                if u == 0:
                    nc.vector.tensor_scalar(h[:, u, 0, P:DIM], h[:, u, 0, P:DIM], keep[:, 0:1], None, ALU.mult)
                    dve.drain()
                norm.statistics(nc, dve, h[:, u, :, :], u)
                norm.inverse(nc, dve, i, u)
                dve.wait_ge(turned.sem, turned.ago(i, u, 2))
                for t in range(CT):
                    last = norm.normalise(nc, hn[:, u, t, :], h[:, u, t, :], u, t)
                last.then_inc(hn_ready.sem, 1)

            def second(i, u):
                for m in range(FM):
                    w = FW[m]
                    if m == 0:
                        dve.wait_ge(summed.sem, summed.ago(i, u, 2))
                    dve.wait_ge(gelu.sem, gelu.of(i, u, m + 1))
                    nc.vector.scalar_tensor_tensor(act_out[0:w, u, m, :], p_ag[0:w, m % 2, 0, :], b1[0:w, 0, m:m + 1],
                                                   gated[0:w, m % 2, :], ALU.add, ALU.mult).then_inc(act_ready.sem, 1)
                dve.wait_ge(rest_ready.sem, rest_ready.of(i, u, 1))
                dve.wait_ge(*stored.before(i, u))
                dve.wait_ge(summed.sem, summed.of(i, u, 1))
                nc.vector.tensor_tensor(z2[:, u, :, :], p_out[:, :, :], rest[:, u, :, :], ALU.add
                                        ).then_inc(z2_ready.sem, 1)

            skewed(dve, pairs, first, second)

        @block.scalar
        def _(act):
            for s in (norm.std_ready, hT_ready, gelu):
                s.prime(act)
            act.wait_ge(norm.eps_ready, 1)
            act.wait_ge(fixed, 16 * (11 + CT))

            def first(i, u):
                norm.deviation(nc, act, i, u)
                act.wait_ge(product.sem, product.ago(i, u, 2))
                act.wait_ge(turned.sem, turned.of(i, u, 1))
                for k in range(KD):
                    last = nc.scalar.activation(hT[:, u, k, :], p_T[:, k, :], ACT.Identity, bias=shift[:, k:k + 1],
                                                scale=gain[:, k:k + 1])
                last.then_inc(hT_ready.sem, 1)

            def second(i, u):
                for m in range(FM):
                    w = FW[m]
                    act.wait_ge(product.sem, product.of(i, u, m + 1))
                    act.wait_ge(act_ready.sem, act_ready.of(i, u, m - 1))
                    nc.scalar.activation(gated[0:w, m % 2, :], p_ag[0:w, m % 2, 1, :], ACT.Gelu,
                                         bias=b1[0:w, 1, m:m + 1]).then_inc(gelu.sem, 1)

            skewed(act, pairs, first, second)

        @block.tensor
        def _(pe):
            for s in (turned, product, summed):
                s.prime(pe)
            pe.wait_ge(fixed, 16 * (11 + CT))

            def first(i, u):
                pe.wait_ge(hn_ready.sem, hn_ready.of(i, u, 1))
                pe.wait_ge(hT_ready.sem, hT_ready.ago(i, u, 1))
                for k in range(KD):
                    for t in range(CT):
                        last = nc.tensor.transpose(p_T[:, k, t * P:(t + 1) * P], hn[:, u, t, k * P:(k + 1) * P],
                                                   ident[:, :])
                last.then_inc(turned.sem, 1)

            def second(i, u):
                pe.wait_ge(hT_ready.sem, hT_ready.of(i, u, 1))
                for m in range(FM):
                    w = FW[m]
                    pe.wait_ge(act_ready.sem, act_ready.of(i, u, m - 1))
                    for n in range(2):
                        for k in range(KD):
                            last = nc.tensor.matmul(p_ag[0:w, m % 2, n, :], w1[:, k, n * HID + m * P:n * HID + m * P + w],
                                                    hT[:, u, k, :], start=k == 0, stop=k == KD - 1)
                    last.then_inc(product.sem, 1)
                pe.wait_ge(act_ready.sem, act_ready.of(i, u, FM))
                pe.wait_ge(z2_ready.sem, z2_ready.ago(i, u, 1))
                for t in range(CT):
                    for m in range(FM):
                        w = FW[m]
                        last = nc.tensor.matmul(p_out[:, t, :], act_out[0:w, u, m, t * P:(t + 1) * P], w2[0:w, m, :],
                                                start=m == 0, stop=m == FM - 1)
                last.then_inc(summed.sem, 1)

            skewed(pe, pairs, first, second)



DI = 2 * DIM
XT = DI // P
NS, RANK = 16, DIM // 16
TAPS = 4


def phase_in_projection(nc, T):
    with ExitStack() as ctx:
        a = Pool_(nc, ctx, "F")
        M = 2 * XT
        ident = a.sb("ident", [P, P])
        w = a.sb("w", [P, KD, 2 * DI])
        x = a.sb("x", [P, 2, CT, DIM])
        xn = a.sb("xn", [P, 2, CT, DIM])
        xT = a.sb("xT", [P, 2, KD, CHUNK])
        xz = a.sb("xz", [P, 2, M, CHUNK])
        p_T = a.ps("p_T", [P, 2, KD, CHUNK])
        p_o = a.ps("p_o", [P, 4, CHUNK])
        norm = Norm(a)
        fixed = a.sem("fixed")
        loaded = a.transfers("loaded")
        xn_ready = a.count("xn_ready", 1)
        turned = a.count("turned", 1)
        xT_ready = a.count("xT_ready", 1)
        product = a.count("product", M)
        x_out = a.count("x_out", XT)
        z_out = a.count("z_out", XT)
        stored = a.transfers("stored", M)
        pairs = CHUNKS // 2
        block = ctx.enter_context(nc.Block())

        @block.sync
        def _(sp):
            gate = Gate(sp, a.sem("passed"))
            for s in (loaded, stored):
                s.prime(sp)
            sp.dma_start(ident[:, :], T["ident"][:, :]).then_inc(fixed, 16)
            sp.dma_start(w[:, :, :], T["w_in"].rearrange("(k p) n -> p k n", p=P)).then_inc(fixed, 16)

            def load(i, u):
                tok = start_of(sp, i, u, CHUNK)
                gate.wait_ge(xn_ready.sem, xn_ready.ago(i, u, 2))
                sp.dma_start(x[:, u, :, :], T["x2"][bass.ds(tok, CHUNK), :].rearrange("(t p) d -> p t d", p=P)
                             ).then_inc(loaded.sems[u], 16)

            def store(i, u):
                row = start_of(sp, i, 0, DI, n=1)
                gate.wait_ge(x_out.sem, x_out.of(i, u, XT))
                gate.wait_ge(z_out.sem, z_out.of(i, u, XT))
                for m in range(M):
                    sp.dma_start(T[("xin", "sz")[m // XT]][bass.ds(row + (m % XT) * P, P), u * CHUNK:(u + 1) * CHUNK],
                                 xz[:, u, m, :]).then_inc(stored.sems[u], 16)

            early(sp, pairs, load, store)
            for u in range(2):
                sp.wait_ge(*stored.done(pairs - 1, u))

        @block.vector
        def _(dve):
            for s in (norm.var_ready, xn_ready, x_out):
                s.prime(dve)
            norm.set_eps(nc, dve)

            def first(i, u):
                dve.wait_ge(*loaded.done(i, u))
                norm.statistics(nc, dve, x[:, u, :, :], u)
                norm.inverse(nc, dve, i, u)
                dve.wait_ge(turned.sem, turned.ago(i, u, 2))
                for t in range(CT):
                    last = norm.normalise(nc, xn[:, u, t, :], x[:, u, t, :], u, t)
                last.then_inc(xn_ready.sem, 1)

            def second(i, u):
                dve.wait_ge(*stored.before(i, u))
                for m in range(XT):
                    dve.wait_ge(product.sem, product.of(i, u, 2 * m + 1))
                    nc.vector.tensor_copy(xz[:, u, m, :], p_o[:, 2 * m % 4, :]).then_inc(x_out.sem, 1)

            skewed(dve, pairs, first, second)

        @block.scalar
        def _(act):
            for s in (norm.std_ready, xT_ready, z_out):
                s.prime(act)
            act.wait_ge(norm.eps_ready, 1)

            def first(i, u):
                norm.deviation(nc, act, i, u)
                act.wait_ge(turned.sem, turned.of(i, u, 1))
                act.wait_ge(product.sem, product.ago(i, u, 2))
                nc.scalar.copy(xT[:, u, :, :], p_T[:, u, :, :]).then_inc(xT_ready.sem, 1)

            def second(i, u):
                act.wait_ge(*stored.before(i, u))
                for m in range(XT):
                    act.wait_ge(product.sem, product.of(i, u, 2 * m + 2))
                    nc.scalar.activation(xz[:, u, XT + m, :], p_o[:, (2 * m + 1) % 4, :], ACT.Silu
                                         ).then_inc(z_out.sem, 1)

            skewed(act, pairs, first, second)

        @block.tensor
        def _(pe):
            turned.prime(pe)
            product.prime(pe)
            pe.wait_ge(fixed, 32)

            def first(i, u):
                pe.wait_ge(xn_ready.sem, xn_ready.of(i, u, 1))
                pe.wait_ge(xT_ready.sem, xT_ready.ago(i, u, 2))
                for k in range(KD):
                    for t in range(CT):
                        last = nc.tensor.transpose(p_T[:, u, k, t * P:(t + 1) * P], xn[:, u, t, k * P:(k + 1) * P],
                                                   ident[:, :])
                last.then_inc(turned.sem, 1)

            def second(i, u):
                pe.wait_ge(xT_ready.sem, xT_ready.of(i, u, 1))
                for n in range(M):
                    m = n // 2 + XT * (n % 2)
                    bank_read = (x_out, z_out)[n % 2]
                    pe.wait_ge(bank_read.sem, bank_read.of(i, u, n // 2 - 1))
                    for k in range(KD):
                        last = nc.tensor.matmul(p_o[:, n % 4, :], w[:, k, m * P:(m + 1) * P], xT[:, u, k, :],
                                                start=k == 0, stop=k == KD - 1)
                    last.then_inc(product.sem, 1)

            skewed(pe, pairs, first, second)



SMALL = 1.0 / 64


def phase_dt(nc, T):
    with ExitStack() as ctx:
        a = Pool_(nc, ctx, "G")
        NR = RANK + 2 * NS
        conv_w = a.sb("conv_w", [P, XT, TAPS])
        conv_b = a.sb("conv_b", [P, XT])
        dt_b = a.sb("dt_b", [P, XT])
        w_x = a.sb("w_x", [P, XT, NR])
        w_dt = a.sb("w_dt", [RANK, DI])
        xin = a.sb("xin", [P, 2, XT, TAPS - 1 + SEQ])
        conv = a.sb("conv", [P, 2, SEQ])
        xs = a.sb("xs", [P, XT, SEQ])
        low = a.sb("low", [NR, SEQ])
        lin = a.sb("lin", [P, 2, SEQ])
        size = a.sb("size", [P, 2, SEQ])
        ex = a.sb("ex", [P, 2, SEQ])
        lg = a.sb("lg", [P, 2, SEQ])
        poly = a.sb("poly", [P, SEQ])
        pick = a.sb("pick", [P, SEQ], I32)
        ndt = a.sb("ndt", [P, XT, SEQ])
        ndu = a.sb("ndu", [P, XT, SEQ])
        p_low = a.ps("p_low", [NR, 2, CHUNK])
        p_dt = a.ps("p_dt", [P, 2, 2, CHUNK])
        fixed = a.sem("fixed")
        U = 1
        loaded = a.count("loaded", 16, U, 1)
        conv_ready = a.count("conv_ready", XT, U, 1)
        xs_ready = a.count("xs_ready", XT, U, 1)
        low_done = a.count("low_done", 1, U, 1)
        low_ready = a.count("low_ready", 1, U, 1)
        dt_done = a.count("dt_done", XT, U, 1)
        log_ready = a.count("log_ready", XT, U, 1)
        ndt_ready = a.count("ndt_ready", XT, U, 1)
        ndu_ready = a.count("ndu_ready", XT, U, 1)
        stored = a.count("stored", 16 * 4, U, 1)
        NFIX = 4 + TAPS
        block = ctx.enter_context(nc.Block())

        @block.sync
        def _(sp):
            gate = Gate(sp, a.sem("passed"))
            loaded.prime(sp)
            stored.prime(sp)
            for out_, in_ in (
                *((conv_w[:, :, j], T["conv_w"][j].rearrange("(m p) -> p m", p=P)) for j in range(TAPS)),
                (conv_b[:, :], T["conv_b"].rearrange("(m p) -> p m", p=P)),
                (dt_b[:, :], T["b_dt"].rearrange("(m p) -> p m", p=P)),
                (w_x[:, :, :], T["w_x"].rearrange("(m p) n -> p m n", p=P)),
                (w_dt[:, :], T["w_dt"][:, :]),
            ):
                sp.dma_start(out_, in_).then_inc(fixed, 16)
            tiles = lambda ap: ap.rearrange("(m p) n -> p m n", p=P)

            def load(i):
                row = start_of(sp, i, 0, DI, n=1)
                gate.wait_ge(conv_ready.sem, conv_ready.ago(i, 0, 1))
                sp.dma_start(xin[:, 0, :, TAPS - 1:TAPS - 1 + SEQ], tiles(T["xin"][bass.ds(row, DI), :])
                             ).then_inc(loaded.sem, 16)

            def store(i, then):
                row = start_of(sp, i, 0, DI, n=1)
                bc = start_of(sp, i, 0, 2 * NS, n=1)
                gate.wait_ge(low_ready.sem, low_ready.of(i, 0, 1))
                sp.dma_start(T["bc"][bass.ds(bc, 2 * NS), :], low[RANK:NR, :]).then_inc(stored.sem, 16)
                gate.wait_ge(xs_ready.sem, xs_ready.of(i, 0, XT))
                sp.dma_start(tiles(T["xs"][bass.ds(row, DI), :]), xs[:, :, :]).then_inc(stored.sem, 16)
                then()
                gate.wait_ge(ndt_ready.sem, ndt_ready.of(i, 0, XT))
                sp.dma_start(tiles(T["ndt"][bass.ds(row, DI), :]), ndt[:, :, :]).then_inc(stored.sem, 16)
                gate.wait_ge(ndu_ready.sem, ndu_ready.of(i, 0, XT))
                sp.dma_start(tiles(T["ndu"][bass.ds(row, DI), :]), ndu[:, :, :]).then_inc(stored.sem, 16)

            load(0)
            with sp.Fori(0, SEQS - 1) as i:
                store(i, lambda: load(i + 1))
            store(SEQS - 1, lambda: None)
            sp.wait_ge(stored.sem, stored.of(SEQS - 1, 0, 64))

        @block.gpsimd
        def _(pool):
            gate = Gate(pool, a.sem("pool_passed"))
            ndu_ready.prime(pool)
            with pool.Fori(0, SEQS) as i:
                gate.wait_ge(stored.sem, stored.ago(i, 0, 1))
                for m in range(XT):
                    gate.wait_ge(ndt_ready.sem, ndt_ready.of(i, 0, m + 1))
                    nc.gpsimd.tensor_tensor(ndu[:, m, :], ndt[:, m, :], xs[:, m, :], ALU.mult
                                            ).then_inc(ndu_ready.sem, 1)

        @block.vector
        def _(dve):
            conv_ready.prime(dve)
            ndt_ready.prime(dve)
            nc.vector.memset(xin[:, :, :, 0:TAPS - 1], 0.0)
            dve.drain()
            dve.wait_ge(fixed, 16 * NFIX)
            with dve.Fori(0, SEQS) as i:
                dve.wait_ge(loaded.sem, loaded.of(i, 0, 16))
                for m in range(XT):
                    dve.wait_ge(xs_ready.sem, xs_ready.of(i, 0, m - 1))
                    nc.vector.tensor_scalar(conv[:, m % 2, :], xin[:, 0, m, 0:SEQ], conv_w[:, m, 0:1], None, ALU.mult)
                    for j in range(1, TAPS):
                        dve.drain()
                        last = nc.vector.scalar_tensor_tensor(conv[:, m % 2, :], xin[:, 0, m, j:j + SEQ],
                                                              conv_w[:, m, j:j + 1], conv[:, m % 2, :],
                                                              ALU.mult, ALU.add)
                    last.then_inc(conv_ready.sem, 1)
                for m in range(XT):
                    e = ex[:, m % 2, :]
                    dve.wait_ge(log_ready.sem, log_ready.of(i, 0, m + 1))
                    nc.vector.tensor_scalar(pick[:, :], e, SMALL, None, ALU.is_lt)
                    nc.vector.tensor_scalar(poly[:, :], e, -0.25, 1.0 / 3, ALU.mult, ALU.add)
                    dve.drain()
                    nc.vector.tensor_tensor(poly[:, :], poly[:, :], e, ALU.mult)
                    for term in (-0.5, 1.0):
                        dve.drain()
                        nc.vector.scalar_tensor_tensor(poly[:, :], poly[:, :], term, e, ALU.add, ALU.mult)
                    dve.drain()
                    nc.vector.copy_predicated(lg[:, m % 2, :], pick[:, :], poly[:, :])
                    dve.drain()
                    if m == 0:
                        dve.wait_ge(stored.sem, stored.ago(i, 0, 1))
                    nc.vector.scalar_tensor_tensor(ndt[:, m, :], lin[:, m % 2, :], 0.0, lg[:, m % 2, :],
                                                   ALU.min, ALU.subtract).then_inc(ndt_ready.sem, 1)

        @block.scalar
        def _(act):
            for s in (xs_ready, low_ready, log_ready):
                s.prime(act)
            act.wait_ge(fixed, 16 * NFIX)
            nc.scalar.mul(dt_b[:, :], dt_b[:, :], -1.0)
            act.drain()
            with act.Fori(0, SEQS) as i:
                act.wait_ge(stored.sem, stored.ago(i, 0, 1))
                for m in range(XT):
                    act.wait_ge(conv_ready.sem, conv_ready.of(i, 0, m + 1))
                    nc.scalar.activation(xs[:, m, :], conv[:, m % 2, :], ACT.Silu, bias=conv_b[:, m:m + 1]
                                         ).then_inc(xs_ready.sem, 1)
                act.wait_ge(low_done.sem, low_done.of(i, 0, 1))
                nc.scalar.copy(low[:, :], p_low[:, :, :].rearrange("p a b -> p (a b)")).then_inc(low_ready.sem, 1)
                for m in range(XT):
                    act.wait_ge(dt_done.sem, dt_done.of(i, 0, m + 1))
                    act.wait_ge(ndt_ready.sem, ndt_ready.of(i, 0, m - 1))
                    src = p_dt[:, m % 2, :, :].rearrange("p a b -> p (a b)")
                    nc.scalar.activation(lin[:, m % 2, :], src, ACT.Identity, bias=dt_b[:, m:m + 1], scale=-1.0)
                    act.drain()
                    nc.scalar.activation(size[:, m % 2, :], lin[:, m % 2, :], ACT.Abs)
                    act.drain()
                    nc.scalar.activation(ex[:, m % 2, :], size[:, m % 2, :], ACT.Exp, scale=-1.0)
                    act.drain()
                    nc.scalar.activation(lg[:, m % 2, :], ex[:, m % 2, :], ACT.Ln, bias=1.0
                                         ).then_inc(log_ready.sem, 1)

        @block.tensor
        def _(pe):
            low_done.prime(pe)
            dt_done.prime(pe)
            pe.wait_ge(fixed, 16 * NFIX)
            with pe.Fori(0, SEQS) as i:
                pe.wait_ge(xs_ready.sem, xs_ready.of(i, 0, XT))
                pe.wait_ge(low_ready.sem, low_ready.ago(i, 0, 1))
                for c in range(2):
                    for m in range(XT):
                        last = nc.tensor.matmul(p_low[:, c, :], w_x[:, m, :], xs[:, m, c * CHUNK:(c + 1) * CHUNK],
                                                start=m == 0, stop=m == XT - 1)
                last.then_inc(low_done.sem, 1)
                pe.wait_ge(low_ready.sem, low_ready.of(i, 0, 1))
                for m in range(XT):
                    pe.wait_ge(log_ready.sem, log_ready.of(i, 0, m - 1))
                    for c in range(2):
                        last = nc.tensor.matmul(p_dt[:, m % 2, c, :], w_dt[:, m * P:(m + 1) * P],
                                                low[0:RANK, c * CHUNK:(c + 1) * CHUNK], start=True, stop=True)
                    last.then_inc(dt_done.sem, 1)




def phase_scan(nc, T):
    with ExitStack() as ctx:
        a = Pool_(nc, ctx, "H")
        units = [(s, m) for s in range(NS) for m in range(XT)]
        NU = len(units)
        ident = a.sb("ident", [P, P])
        rate = a.sb("rate", [P, XT, NS])
        skip = a.sb("skip", [P, XT])
        ndt = a.sb("ndt", [P, XT, SEQ])
        ndu = a.sb("ndu", [P, XT, SEQ])
        xs = a.sb("xs", [P, XT, SEQ])
        sz = a.sb("sz", [P, XT, SEQ])
        bs = a.sb("bs", [P, 2, SEQ])
        cs = a.sb("cs", [P, 2, SEQ])
        decay = a.sb("decay", [P, 3, SEQ])
        feed = a.sb("feed", [P, 3, SEQ])
        state = a.sb("state", [P, 2, SEQ])
        part = a.sb("part", [P, 3, SEQ])
        yg = a.sb("yg", [P, XT, SEQ])
        p_y = a.ps("p_y", [P, XT, 2, CHUNK])
        fixed = a.sem("fixed")
        rate_ready = a.sem("rate_ready")
        loaded = a.count("loaded", 16 * 2, 1, 1)
        tail_loaded = a.count("tail_loaded", 16 * 2, 1, 1)
        row_loaded = [a.count(f"row_loaded_{n}", 16 * 2 * (NS // 2), 1, 1) for n in range(2)]
        decayed = a.count("decayed", NU, 1, 1)
        fed = a.count("fed", NU, 1, 1)
        scanned = a.count("scanned", NU, 1, 1)
        parted = a.count("parted", NU, 1, 1)
        summed = a.count("summed", NU, 1, 1)
        yg_ready = a.count("yg_ready", XT, 1, 1)
        stored = a.count("stored", 16, 1, 1)
        NFIX = 3
        block = ctx.enter_context(nc.Block())

        @block.sync
        def _(sp):
            gate = Gate(sp, a.sem("passed"))
            for s in (loaded, tail_loaded, stored, *row_loaded):
                s.prime(sp)
            sp.dma_start(ident[:, :], T["ident"][:, :]).then_inc(fixed, 16)
            sp.dma_start(rate[:, :, :], T["a_log"].rearrange("(m p) s -> p m s", p=P)).then_inc(fixed, 16)
            sp.dma_start(skip[:, :], T["d"].rearrange("(m p) -> p m", p=P)).then_inc(fixed, 16)
            tiles = lambda ap: ap.rearrange("(m p) n -> p m n", p=P)

            def load(i):
                row = start_of(sp, i, 0, DI, n=1)
                gate.wait_ge(scanned.sem, scanned.ago(i, 0, 1))
                sp.dma_start(ndt[:, :, :], tiles(T["ndt"][bass.ds(row, DI), :])).then_inc(loaded.sem, 16)
                sp.dma_start(ndu[:, :, :], tiles(T["ndu"][bass.ds(row, DI), :])).then_inc(loaded.sem, 16)

            def rows(i):
                row = start_of(sp, i, 0, DI, n=1)
                bc = start_of(sp, i, 0, 2 * NS, n=1)
                for s in range(NS):
                    gate.wait_ge(parted.sem, parted.of(i, 0, XT * (s - 1)))
                    sp.dma_start(bs[:, s % 2, :], T["bc"][bass.ds(bc + s, 1), :].broadcast_to([P, SEQ])
                                 ).then_inc(row_loaded[s % 2].sem, 16)
                    sp.dma_start(cs[:, s % 2, :], T["bc"][bass.ds(bc + NS + s, 1), :].broadcast_to([P, SEQ])
                                 ).then_inc(row_loaded[s % 2].sem, 16)
                    if s == 2:
                        gate.wait_ge(yg_ready.sem, yg_ready.ago(i, 0, 1))
                        sp.dma_start(xs[:, :, :], tiles(T["xs"][bass.ds(row, DI), :])).then_inc(tail_loaded.sem, 16)
                        sp.dma_start(sz[:, :, :], tiles(T["sz"][bass.ds(row, DI), :])).then_inc(tail_loaded.sem, 16)

            def store(i):
                row = start_of(sp, i, 0, DI, n=1)
                gate.wait_ge(yg_ready.sem, yg_ready.of(i, 0, XT))
                sp.dma_start(tiles(T["ygT"][bass.ds(row, DI), :]), yg[:, :, :]).then_inc(stored.sem, 16)

            load(0)
            with sp.Fori(0, SEQS - 1) as i:
                rows(i)
                load(i + 1)
                store(i)
            rows(SEQS - 1)
            store(SEQS - 1)
            sp.wait_ge(stored.sem, stored.of(SEQS - 1, 0, 16))

        @block.scalar
        def _(act):
            decayed.prime(act)
            act.wait_ge(fixed, 16 * NFIX)
            nc.scalar.activation(rate[:, :, :], rate[:, :, :], ACT.Exp)
            act.drain()
            with act.Fori(0, SEQS) as i:
                act.wait_ge(loaded.sem, loaded.of(i, 0, 32))
                for n, (s, m) in enumerate(units):
                    act.wait_ge(scanned.sem, scanned.of(i, 0, n - 2))
                    nc.scalar.activation(decay[:, n % 3, :], ndt[:, m, :], ACT.Exp, scale=rate[:, m, s:s + 1]
                                         ).then_inc(decayed.sem, 1)

        @block.gpsimd
        def _(pool):
            gate = Gate(pool, a.sem("pool_passed"))
            fed.prime(pool)
            with pool.Fori(0, SEQS) as i:
                gate.wait_ge(loaded.sem, loaded.of(i, 0, 32))
                for n, (s, m) in enumerate(units):
                    if m == 0:
                        rows = row_loaded[s % 2]
                        gate.wait_ge(rows.sem, rows.of(i, 0, 32 * (s // 2 + 1)))
                    gate.wait_ge(scanned.sem, scanned.of(i, 0, n - 2))
                    nc.gpsimd.tensor_tensor(feed[:, n % 3, :], ndu[:, m, :], bs[:, s % 2, :], ALU.mult
                                            ).then_inc(fed.sem, 1)

        @block.vector
        def _(dve):
            for s in (scanned, parted, yg_ready):
                s.prime(dve)
            dve.wait_ge(fixed, 16 * NFIX)
            with dve.Fori(0, SEQS) as i:
                def times_c(n):
                    s, m = units[n]
                    dve.wait_ge(scanned.sem, scanned.of(i, 0, n + 1))
                    dve.wait_ge(summed.sem, summed.of(i, 0, n - 2))
                    nc.vector.scalar_tensor_tensor(part[:, n % 3, :], state[:, n % 2, :], -1.0, cs[:, s % 2, :],
                                                   ALU.mult, ALU.mult).then_inc(parted.sem, 1)

                for n, (s, m) in enumerate(units):
                    dve.wait_ge(decayed.sem, decayed.of(i, 0, n + 1))
                    dve.wait_ge(fed.sem, fed.of(i, 0, n + 1))
                    dve.wait_ge(parted.sem, parted.of(i, 0, n - 1))
                    nc.vector.tensor_tensor_scan(state[:, n % 2, :], decay[:, n % 3, :], feed[:, n % 3, :], 0.0,
                                                 ALU.mult, ALU.add).then_inc(scanned.sem, 1)
                    if m == 0:
                        rows = row_loaded[s % 2]
                        dve.wait_ge(rows.sem, rows.of(i, 0, 32 * (s // 2 + 1)))
                    if n:
                        times_c(n - 1)
                times_c(NU - 1)
                dve.wait_ge(tail_loaded.sem, tail_loaded.of(i, 0, 32))
                dve.wait_ge(stored.sem, stored.ago(i, 0, 1))
                for m in range(XT):
                    dve.wait_ge(summed.sem, summed.of(i, 0, NU - XT + m + 1))
                    nc.vector.scalar_tensor_tensor(yg[:, m, :], xs[:, m, :], skip[:, m:m + 1],
                                                   p_y[:, m, :, :].rearrange("p a b -> p (a b)"), ALU.mult, ALU.add)
                dve.drain()
                for m in range(XT):
                    nc.vector.tensor_tensor(yg[:, m, :], yg[:, m, :], sz[:, m, :], ALU.mult
                                            ).then_inc(yg_ready.sem, 1)

        @block.tensor
        def _(pe):
            summed.prime(pe)
            pe.wait_ge(fixed, 16 * NFIX)
            with pe.Fori(0, SEQS) as i:
                for n, (s, m) in enumerate(units):
                    if s == 0:
                        pe.wait_ge(yg_ready.sem, yg_ready.ago(i, 0, 1))
                    pe.wait_ge(parted.sem, parted.of(i, 0, n + 1))
                    for c in range(2):
                        last = nc.tensor.matmul(p_y[:, m, c, :], ident[:, :],
                                                part[:, n % 3, c * CHUNK:(c + 1) * CHUNK],
                                                start=s == 0, stop=s == NS - 1)
                    last.then_inc(summed.sem, 1)



EXPERTS = 32
CAPACITY = int(-(-1.25 * TOKENS // EXPERTS))
SLOTS = EXPERTS * CAPACITY


def phase_router(nc, T):
    with ExitStack() as ctx:
        a = Pool_(nc, ctx, "I")
        ident = a.sb("ident", [P, P])
        w = a.sb("w", [P, XT, DIM])
        w_r = a.sb("w_r", [P, KD, EXPERTS])
        number = a.sb("number", [P, CT, EXPERTS])
        zeros = a.sb("zeros", [P, SLOTS // P // 4 * DIM])
        ygT = a.sb("ygT", [P, 2, XT, CHUNK])
        x = a.sb("x", [P, 2, CT, DIM])
        x3 = a.sb("x3", [P, 2, CT, DIM])
        xt = a.sb("xt", [P, 2, CT, DIM])
        base = a.sb("base", [P, 2, CT, DIM])
        xT = a.sb("xT", [P, 2, KD, CHUNK])
        top = a.sb("top", [P, 2, CT])
        ntop = a.sb("ntop", [P, 2, CT])
        ex = a.sb("ex", [P, 2, CT, EXPERTS])
        total = a.sb("total", [P, 2, CT])
        equal = a.sb("equal", [P, 2, CT, EXPERTS])
        first_ = a.sb("first_", [P, 2, CT])
        chosen = a.sb("chosen", [P, 2, CT, EXPERTS])
        meta = a.sb("meta", [P, 2, CT, 2])
        p_out = a.ps("p_out", [P, 2, CT, DIM])
        p_T = a.ps("p_T", [P, KD, CHUNK])
        p_log = a.ps("p_log", [P, 2, 512])
        norm = Norm(a)
        fixed = a.sem("fixed")
        zeros_ready = a.sem("zeros_ready")
        zeroed = a.sem("zeroed")
        loaded = a.transfers("loaded", 2)
        product = a.count("product", 1)
        x3_ready = a.count("x3_ready", 1)
        xt_ready = a.count("xt_ready", 1)
        base_ready = a.count("base_ready", 1)
        turned = a.count("turned", 1)
        xT_ready = a.count("xT_ready", 1)
        routed = a.count("routed", 1)
        top_ready = a.count("top_ready", 1)
        ex_ready = a.count("ex_ready", 1)
        meta_ready = a.count("meta_ready", 1)
        stored = a.transfers("stored", 4)
        pairs = CHUNKS // 2
        block = ctx.enter_context(nc.Block())

        @block.sync
        def _(sp):
            gate = Gate(sp, a.sem("passed"))
            loaded.prime(sp)
            stored.prime(sp)
            sp.dma_start(ident[:, :], T["ident"][:, :]).then_inc(fixed, 16)
            sp.dma_start(w[:, :, :], T["w_out"].rearrange("(k p) n -> p k n", p=P)).then_inc(fixed, 16)
            sp.dma_start(w_r[:, :, :], T["w_router"].rearrange("(k p) n -> p k n", p=P)).then_inc(fixed, 16)
            for t in range(CT):
                sp.dma_start(number[:, t, :], T["numbers"][:, :]).then_inc(fixed, 16)
            tiles = lambda ap: ap.rearrange("(t p) d -> p t d", p=P)

            def load(i, u):
                tok = start_of(sp, i, u, CHUNK)
                row = start_of(sp, i, 0, DI, n=1)
                gate.wait_ge(product.sem, product.ago(i, u, 2))
                sp.dma_start(ygT[:, u, :, :], T["ygT"][bass.ds(row, DI), u * CHUNK:(u + 1) * CHUNK]
                             .rearrange("(k p) n -> p k n", p=P)).then_inc(loaded.sems[u], 16)
                gate.wait_ge(x3_ready.sem, x3_ready.ago(i, u, 2))
                sp.dma_start(x[:, u, :, :], tiles(T["x2"][bass.ds(tok, CHUNK), :])).then_inc(loaded.sems[u], 16)

            def store(i, u):
                tok = start_of(sp, i, u, CHUNK)
                gate.wait_ge(xt_ready.sem, xt_ready.of(i, u, 1))
                sp.dma_start(tiles(T["xt"][bass.ds(tok, CHUNK), :]), xt[:, u, :, :]).then_inc(stored.sems[u], 16)
                gate.wait_ge(base_ready.sem, base_ready.of(i, u, 1))
                sp.dma_start(tiles(T["base"][bass.ds(tok, CHUNK), :]), base[:, u, :, :]).then_inc(stored.sems[u], 16)
                gate.wait_ge(meta_ready.sem, meta_ready.of(i, u, 1))
                sp.dma_start(tiles(T["chosen"][bass.ds(tok, CHUNK), :]), chosen[:, u, :, :]
                             ).then_inc(stored.sems[u], 16)
                sp.dma_start(tiles(T["meta"][bass.ds(tok, CHUNK), :]), meta[:, u, :, :]).then_inc(stored.sems[u], 16)

            early(sp, pairs, load, store)
            for u in range(2):
                sp.wait_ge(*stored.done(pairs - 1, u))

        @block.gpsimd
        def _(pool):
            gate = Gate(pool, a.sem("pool_passed"))
            base_ready.prime(pool)
            nc.gpsimd.memset(zeros[:, :], 0.0).then_inc(zeros_ready, 1)
            with pool.Fori(0, pairs) as i:
                for u in range(2):
                    gate.wait_ge(xt_ready.sem, xt_ready.of(i, u, 1))
                    gate.wait_ge(*stored.before(i, u))
                    nc.gpsimd.tensor_tensor(base[:, u, :, :], x3[:, u, :, :], xt[:, u, :, :], ALU.add
                                            ).then_inc(base_ready.sem, 1)

        @block.vector
        def _(dve):
            for s in (norm.var_ready, x3_ready, xt_ready, top_ready, meta_ready):
                s.prime(dve)
            norm.set_eps(nc, dve)
            dve.wait_ge(fixed, 16 * (3 + CT))

            def first(i, u):
                dve.wait_ge(product.sem, product.of(i, u, 1))
                dve.wait_ge(*loaded.done(i, u))
                dve.wait_ge(base_ready.sem, base_ready.ago(i, u, 2))
                nc.vector.tensor_tensor(x3[:, u, :, :], p_out[:, u, :, :], x[:, u, :, :], ALU.add
                                        ).then_inc(x3_ready.sem, 1)
                dve.drain()
                norm.statistics(nc, dve, x3[:, u, :, :], u)
                norm.inverse(nc, dve, i, u)
                dve.wait_ge(*stored.before(i, u))
                for t in range(CT):
                    last = norm.normalise(nc, xt[:, u, t, :], x3[:, u, t, :], u, t)
                last.then_inc(xt_ready.sem, 1)

            def second(i, u):
                logits = p_log[:, u, 0:CT * EXPERTS].rearrange("p (t e) -> p t e", t=CT)
                wide = lambda ap: ap.rearrange("p (t e) -> p t e", e=1).broadcast_to([P, CT, EXPERTS])
                dve.wait_ge(routed.sem, routed.of(i, u, 1))
                nc.vector.tensor_reduce(top[:, u, :], logits, AX.X, ALU.max)
                dve.drain()
                nc.vector.tensor_scalar(ntop[:, u, :], top[:, u, :], -1.0, None, ALU.mult)
                nc.vector.tensor_tensor(equal[:, u, :, :], logits, wide(top[:, u, :]), ALU.is_equal
                                        ).then_inc(top_ready.sem, 1)
                dve.drain()
                nc.vector.tensor_tensor(equal[:, u, :, :], equal[:, u, :, :], number[:, :, :], ALU.mult)
                dve.drain()
                nc.vector.tensor_reduce(first_[:, u, :], equal[:, u, :, :], AX.X, ALU.min)
                dve.drain()
                dve.wait_ge(*stored.before(i, u))
                nc.vector.tensor_tensor(chosen[:, u, :, :], number[:, :, :], wide(first_[:, u, :]), ALU.is_equal)
                nc.vector.tensor_scalar(meta[:, u, :, 0], first_[:, u, :], float(EXPERTS), None, ALU.add)
                dve.wait_ge(ex_ready.sem, ex_ready.of(i, u, 1))
                nc.vector.reciprocal(meta[:, u, :, 1], total[:, u, :]).then_inc(meta_ready.sem, 1)

            skewed(dve, pairs, first, second)

        @block.scalar
        def _(act):
            for s in (norm.std_ready, xT_ready, ex_ready):
                s.prime(act)
            act.wait_ge(norm.eps_ready, 1)
            act.wait_ge(zeros_ready, 1)
            rows = SLOTS // 4
            for n in range(4):
                act.dma_start(T["slots_x"][n * rows:(n + 1) * rows, :].rearrange("(p t) d -> p (t d)", p=P),
                              zeros[:, :]).then_inc(zeroed, 16)

            def first(i, u):
                norm.deviation(nc, act, i, u)

            def second(i, u):
                act.wait_ge(turned.sem, turned.of(i, u, 1))
                act.wait_ge(routed.sem, routed.ago(i, u, 2))
                nc.scalar.copy(xT[:, u, :, :], p_T[:, :, :]).then_inc(xT_ready.sem, 1)
                act.wait_ge(top_ready.sem, top_ready.of(i, u, 1))
                act.wait_ge(meta_ready.sem, meta_ready.ago(i, u, 2))
                for t in range(CT):
                    last = nc.scalar.activation(ex[:, u, t, :], p_log[:, u, t * EXPERTS:(t + 1) * EXPERTS], ACT.Exp,
                                                bias=ntop[:, u, t:t + 1], accum_out=total[:, u, t:t + 1])
                last.then_inc(ex_ready.sem, 1)

            skewed(act, pairs, first, second)
            act.wait_ge(zeroed, 64)

        @block.tensor
        def _(pe):
            for s in (product, turned, routed):
                s.prime(pe)
            pe.wait_ge(fixed, 16 * (3 + CT))

            def first(i, u):
                pe.wait_ge(*loaded.done(i, u))
                pe.wait_ge(x3_ready.sem, x3_ready.ago(i, u, 2))
                for t in range(CT):
                    for k in range(XT):
                        last = nc.tensor.matmul(p_out[:, u, t, :], ygT[:, u, k, t * P:(t + 1) * P], w[:, k, :],
                                                start=k == 0, stop=k == XT - 1)
                last.then_inc(product.sem, 1)

            def second(i, u):
                pe.wait_ge(xt_ready.sem, xt_ready.of(i, u, 1))
                pe.wait_ge(xT_ready.sem, xT_ready.ago(i, u, 1))
                for k in range(KD):
                    for t in range(CT):
                        last = nc.tensor.transpose(p_T[:, k, t * P:(t + 1) * P], xt[:, u, t, k * P:(k + 1) * P],
                                                   ident[:, :])
                last.then_inc(turned.sem, 1)
                pe.wait_ge(xT_ready.sem, xT_ready.of(i, u, 1))
                pe.wait_ge(meta_ready.sem, meta_ready.ago(i, u, 2))
                for t in range(CT):
                    for k in range(KD):
                        last = nc.tensor.matmul(p_log[:, u, t * EXPERTS:(t + 1) * EXPERTS],
                                                xT[:, u, k, t * P:(t + 1) * P], w_r[:, k, :],
                                                start=k == 0, stop=k == KD - 1)
                last.then_inc(routed.sem, 1)

            skewed(pe, pairs, first, second)




def slot_tables():
    upto = (np.arange(P)[:, None] <= np.arange(P)[None]).astype(np.float32)
    token = (np.arange(TILES)[None] * P + np.arange(P)[:, None] + SLOTS).astype(np.float32)
    numbers = np.tile(np.arange(EXPERTS, dtype=np.float32) - EXPERTS, (P, 1))
    return {"upto": upto, "spare": token, "numbers": numbers}


def phase_slots(nc, T):
    with ExitStack() as ctx:
        a = Pool_(nc, ctx, "J")
        N = TILES * EXPERTS
        upto = a.sb("upto", [P, P])
        ones = a.sb("ones", [P, P])
        spare = a.sb("spare", [P, TILES])
        chosen = a.sb("chosen", [P, N])
        meta = a.sb("meta", [P, TILES, 2])
        ahead = a.sb("ahead", [P, 2, N])
        rank = a.sb("rank", [P, N])
        rank_own = a.sb("rank_own", [P, TILES])
        fits = a.sb("fits", [P, TILES])
        slot = a.sb("slot", [P, TILES])
        slot_to = a.sb("slot_to", [P, TILES])
        slot_int = a.sb("slot_int", [P, TILES], I32)
        from_int = a.sb("from_int", [P, TILES], I32)
        weight = a.sb("weight", [P, TILES])
        p_rank = a.ps("p_rank", [P, N])
        p_count = a.ps("p_count", [P, N])
        loaded = a.sem("loaded")
        ones_ready = a.sem("ones_ready")
        counted = a.sem("counted")
        slots_ready = a.sem("slots_ready")
        stored = a.sem("stored")
        block = ctx.enter_context(nc.Block())

        @block.sync
        def _(sp):
            for out_, in_ in (
                (upto[:, :], T["upto"][:, :]), (spare[:, :], T["spare"][:, :]),
                (chosen[:, :].rearrange("p (t e) -> p t e", t=TILES), T["chosen"].rearrange("(t p) e -> p t e", p=P)),
                (meta[:, :, :], T["meta"].rearrange("(t p) e -> p t e", p=P)),
            ):
                sp.dma_start(out_, in_).then_inc(loaded, 16)
            sp.wait_ge(slots_ready, 1)
            for out_, in_ in ((T["slot_to"], slot_int), (T["slot_from"], from_int), (T["weight"], weight)):
                sp.dma_start(out_[:, :], in_[:, :]).then_inc(stored, 16)
            sp.wait_ge(stored, 48)

        @block.tensor
        def _(pe):
            pe.wait_ge(loaded, 64)
            pe.wait_ge(ones_ready, 1)
            for c in range(N // 512):
                part = slice(512 * c, 512 * c + 512)
                nc.tensor.matmul(p_rank[:, part], upto[:, :], chosen[:, part], start=True, stop=True)
                last = nc.tensor.matmul(p_count[:, part], ones[:, :], chosen[:, part], start=True, stop=True)
            last.then_inc(counted, 1)

        @block.vector
        def _(dve):
            nc.vector.memset(ones[:, :], 1.0).then_inc(ones_ready, 1)
            nc.vector.memset(ahead[:, 0, 0:EXPERTS], 0.0)
            dve.wait_ge(counted, 1)
            nc.vector.tensor_copy(ahead[:, 0, EXPERTS:N], p_count[:, 0:N - EXPERTS])
            side, step = 0, EXPERTS
            while step < N:
                dve.drain()
                nc.vector.tensor_copy(ahead[:, 1 - side, 0:step], ahead[:, side, 0:step])
                nc.vector.tensor_tensor(ahead[:, 1 - side, step:N], ahead[:, side, step:N],
                                        ahead[:, side, 0:N - step], ALU.add)
                side, step = 1 - side, 2 * step
            dve.drain()
            nc.vector.tensor_tensor(rank[:, :], p_rank[:, :], ahead[:, side, :], ALU.add)
            dve.drain()
            dve.wait_ge(loaded, 64)
            nc.vector.scalar_tensor_tensor(rank[:, :], rank[:, :], 1.0, chosen[:, :], ALU.subtract, ALU.mult)
            dve.drain()
            nc.vector.tensor_reduce(rank_own[:, :], rank[:, :].rearrange("p (t e) -> p t e", t=TILES), AX.X, ALU.add)
            dve.drain()
            nc.vector.tensor_scalar(fits[:, :], rank_own[:, :], float(CAPACITY), None, ALU.is_lt)
            nc.vector.scalar_tensor_tensor(slot[:, :], meta[:, :, 0], float(CAPACITY), rank_own[:, :],
                                           ALU.mult, ALU.add)
            dve.drain()
            nc.vector.tensor_tensor(slot[:, :], slot[:, :], spare[:, :], ALU.subtract)
            nc.vector.tensor_tensor(weight[:, :], meta[:, :, 1], fits[:, :], ALU.mult)
            dve.drain()
            nc.vector.tensor_tensor(slot[:, :], slot[:, :], fits[:, :], ALU.mult)
            dve.drain()
            nc.vector.tensor_tensor(slot_to[:, :], slot[:, :], spare[:, :], ALU.add)
            dve.drain()
            nc.vector.tensor_copy(slot_int[:, :], slot_to[:, :])
            nc.vector.tensor_scalar(from_int[:, :], slot_to[:, :], float(SLOTS - 1), None, ALU.min)
            dve.drain().then_inc(slots_ready, 1)




def phase_scatter(nc, T):
    with ExitStack() as ctx:
        a = Pool_(nc, ctx, "K")
        xt = a.sb("xt", [P, 2, DIM])
        slot = a.sb("slot", [P, 2, 1], I32)
        loaded = a.transfers("loaded", 2)
        sent = [a.sem(f"sent_{u}") for u in range(2)]
        pairs = TILES // 2
        block = ctx.enter_context(nc.Block())

        @block.sync
        def _(sp):
            gate = Gate(sp, a.sem("passed"))
            loaded.prime(sp)

            def load(i, u, again):
                tok = start_of(sp, i, u, P)
                col = start_of(sp, i, u, 1)
                if again:
                    gate.wait_ge(sent[u], i * 16)
                sp.dma_start(xt[:, u, :], T["xt"][bass.ds(tok, P), :]).then_inc(loaded.sems[u], 16)
                sp.dma_start(slot[:, u, :], T["slot_to"][:, bass.ds(col, 1)]).then_inc(loaded.sems[u], 16)

            for u in range(2):
                load(0, u, False)
            with sp.Fori(1, pairs) as i:
                for u in range(2):
                    load(i, u, True)

        @block.gpsimd
        def _(pool):
            gate = Gate(pool, a.sem("pool_passed"))
            with pool.Fori(0, pairs) as i:
                for u in range(2):
                    gate.wait_ge(*loaded.done(i, u))
                    pool.indirect_dma_start(T["slots_x"][:, :], bass.IndirectOffsetOnAxis(slot[:, u, :], axis=0),
                                            xt[:, u, :], None).then_inc(sent[u], 16)
            for u in range(2):
                pool.wait_ge(sent[u], 16 * pairs)




def phase_experts(nc, T):
    with ExitStack() as ctx:
        a = Pool_(nc, ctx, "L")
        REST = CAPACITY - P
        ident = a.sb("ident", [P, P])
        x = a.sb("x", [P, 2, 2, DIM])
        wg = a.sb("wg", [P, 2, KD, DIM])
        wu = a.sb("wu", [P, 2, KD, DIM])
        wd = a.sb("wd", [P, 2, KD, DIM])
        xT = a.sb("xT", [P, 2, KD, CAPACITY])
        sg = a.sb("sg", [P, 2, KD, CAPACITY])
        hidden = a.sb("hidden", [P, 2, KD, CAPACITY])
        y = a.sb("y", [P, 2, 2, DIM])
        p_T = a.ps("p_T", [P, 2, 512])
        p_g = a.ps("p_g", [P, 2, 512])
        p_u = a.ps("p_u", [P, 2, 512])
        p_y = a.ps("p_y", [P, 2, 2, DIM])
        fixed = a.sem("fixed")
        x_loaded = a.transfers("x_loaded", 2)
        w_loaded = a.transfers("w_loaded", 3)
        turned = a.count("turned", 1)
        xT_ready = a.count("xT_ready", 1)
        gate_up = a.count("gate_up", 1)
        silu = a.count("silu", 1)
        hidden_ready = a.count("hidden_ready", 1)
        down = a.count("down", 1)
        y_ready = a.count("y_ready", 1)
        stored = a.transfers("stored", 2)
        pairs = EXPERTS // 2
        block = ctx.enter_context(nc.Block())

        @block.sync
        def _(sp):
            gate = Gate(sp, a.sem("passed"))
            for s in (x_loaded, w_loaded, stored):
                s.prime(sp)
            sp.dma_start(ident[:, :], T["ident"][:, :]).then_inc(fixed, 16)

            def load(i, u):
                row = start_of(sp, i, u, CAPACITY)
                e = start_of(sp, i, u, DIM)
                gate.wait_ge(gate_up.sem, gate_up.ago(i, u, 2))
                sp.dma_start(x[:, u, 0, :], T["slots_x"][bass.ds(row, P), :]).then_inc(x_loaded.sems[u], 16)
                sp.dma_start(x[0:REST, u, 1, :], T["slots_x"][bass.ds(row + P, REST), :]
                             ).then_inc(x_loaded.sems[u], 16)
                for dst, src in ((wg, "w_gate"), (wu, "w_up"), (wd, "w_down")):
                    if dst is wd:
                        gate.wait_ge(down.sem, down.ago(i, u, 2))
                    sp.dma_start(dst[:, u, :, :], T[src][bass.ds(e, DIM), :].rearrange("(k p) n -> p k n", p=P)
                                 ).then_inc(w_loaded.sems[u], 16)

            def store(i, u):
                row = start_of(sp, i, u, CAPACITY)
                gate.wait_ge(y_ready.sem, y_ready.of(i, u, 1))
                sp.dma_start(T["slots_y"][bass.ds(row, P), :], y[:, u, 0, :]).then_inc(stored.sems[u], 16)
                sp.dma_start(T["slots_y"][bass.ds(row + P, REST), :], y[0:REST, u, 1, :]
                             ).then_inc(stored.sems[u], 16)

            early(sp, pairs, load, store)
            for u in range(2):
                sp.wait_ge(*stored.done(pairs - 1, u))

        @block.vector
        def _(dve):
            hidden_ready.prime(dve)
            y_ready.prime(dve)

            def first(i, u):
                dve.wait_ge(silu.sem, silu.of(i, u, 1))
                dve.wait_ge(down.sem, down.ago(i, u, 2))
                nc.vector.tensor_tensor(hidden[:, u, :, :].rearrange("p k n -> p (k n)"),
                                        sg[:, u, :, :].rearrange("p k n -> p (k n)"),
                                        p_u[:, u, 0:KD * CAPACITY], ALU.mult).then_inc(hidden_ready.sem, 1)

            def second(i, u):
                dve.wait_ge(down.sem, down.of(i, u, 1))
                dve.wait_ge(*stored.before(i, u))
                nc.vector.tensor_copy(y[:, u, 0, :], p_y[:, u, 0, :])
                nc.vector.tensor_copy(y[0:REST, u, 1, :], p_y[0:REST, u, 1, :]).then_inc(y_ready.sem, 1)

            skewed(dve, pairs, first, second)

        @block.scalar
        def _(act):
            xT_ready.prime(act)
            silu.prime(act)
            with act.Fori(0, pairs) as i:
                for u in range(2):
                    act.wait_ge(turned.sem, turned.of(i, u, 1))
                    act.wait_ge(gate_up.sem, gate_up.ago(i, u, 2))
                    nc.scalar.copy(xT[:, u, :, :].rearrange("p k n -> p (k n)"), p_T[:, u, 0:KD * CAPACITY]
                                   ).then_inc(xT_ready.sem, 1)
                    act.wait_ge(gate_up.sem, gate_up.of(i, u, 1))
                    act.wait_ge(hidden_ready.sem, hidden_ready.ago(i, u, 2))
                    nc.scalar.activation(sg[:, u, :, :].rearrange("p k n -> p (k n)"), p_g[:, u, 0:KD * CAPACITY],
                                         ACT.Silu).then_inc(silu.sem, 1)

        @block.tensor
        def _(pe):
            for s in (turned, gate_up, down):
                s.prime(pe)
            pe.wait_ge(fixed, 16)

            def first(i, u):
                pe.wait_ge(*x_loaded.done(i, u))
                pe.wait_ge(xT_ready.sem, xT_ready.ago(i, u, 2))
                for k in range(KD):
                    cols = slice(k * P, (k + 1) * P)
                    at = k * CAPACITY
                    nc.tensor.transpose(p_T[:, u, at:at + P], x[:, u, 0, cols], ident[:, :])
                    last = nc.tensor.transpose(p_T[:, u, at + P:at + CAPACITY], x[0:REST, u, 1, cols],
                                               ident[0:REST, 0:REST])
                last.then_inc(turned.sem, 1)
                pe.wait_ge(xT_ready.sem, xT_ready.of(i, u, 1))
                pe.wait_ge(*w_loaded.done(i, u))
                pe.wait_ge(hidden_ready.sem, hidden_ready.ago(i, u, 2))
                for w, p in ((wg, p_g), (wu, p_u)):
                    for m in range(KD):
                        for k in range(KD):
                            last = nc.tensor.matmul(p[:, u, m * CAPACITY:(m + 1) * CAPACITY],
                                                    w[:, u, k, m * P:(m + 1) * P], xT[:, u, k, :],
                                                    start=k == 0, stop=k == KD - 1)
                last.then_inc(gate_up.sem, 1)

            def second(i, u):
                pe.wait_ge(hidden_ready.sem, hidden_ready.of(i, u, 1))
                pe.wait_ge(y_ready.sem, y_ready.ago(i, u, 2))
                for t, rows in enumerate((P, REST)):
                    for k in range(KD):
                        last = nc.tensor.matmul(p_y[0:rows, u, t, :], hidden[:, u, k, t * P:t * P + rows],
                                                wd[:, u, k, :], start=k == 0, stop=k == KD - 1)
                last.then_inc(down.sem, 1)

            skewed(pe, pairs, first, second)




def phase_combine(nc, T):
    with ExitStack() as ctx:
        a = Pool_(nc, ctx, "M")
        slot = a.sb("slot", [P, 2, 1], I32)
        weight = a.sb("weight", [P, TILES])
        wcol = a.sb("wcol", [P, 2, 1])
        base = a.sb("base", [P, 2, DIM])
        y = a.sb("y", [P, 2, DIM])
        out = a.sb("out", [P, 2, DIM])
        loaded = a.transfers("loaded", 3)
        fetched = [a.sem(f"fetched_{u}") for u in range(2)]
        out_ready = a.count("out_ready", 1)
        stored = a.transfers("stored")
        pairs = TILES // 2
        block = ctx.enter_context(nc.Block())

        @block.sync
        def _(sp):
            gate = Gate(sp, a.sem("passed"))
            loaded.prime(sp)
            stored.prime(sp)

            def load(i, u):
                tok = start_of(sp, i, u, P)
                col = start_of(sp, i, u, 1)
                gate.wait_ge(out_ready.sem, out_ready.ago(i, u, 2))
                sp.dma_start(slot[:, u, :], T["slot_from"][:, bass.ds(col, 1)]).then_inc(loaded.sems[u], 16)
                sp.dma_start(wcol[:, u, :], T["weight"][:, bass.ds(col, 1)]).then_inc(loaded.sems[u], 16)
                sp.dma_start(base[:, u, :], T["base"][bass.ds(tok, P), :]).then_inc(loaded.sems[u], 16)

            def store(i, u):
                tok = start_of(sp, i, u, P)
                gate.wait_ge(out_ready.sem, out_ready.of(i, u, 1))
                sp.dma_start(T["out"][bass.ds(tok, P), :], out[:, u, :]).then_inc(stored.sems[u], 16)

            early(sp, pairs, load, store)
            for u in range(2):
                sp.wait_ge(*stored.done(pairs - 1, u))

        @block.gpsimd
        def _(pool):
            gate = Gate(pool, a.sem("pool_passed"))
            with pool.Fori(0, pairs) as i:
                for u in range(2):
                    gate.wait_ge(*loaded.done(i, u))
                    pool.indirect_dma_start(y[:, u, :], None, T["slots_y"][:, :],
                                            bass.IndirectOffsetOnAxis(slot[:, u, :], axis=0)).then_inc(fetched[u], 16)

        @block.vector
        def _(dve):
            out_ready.prime(dve)
            with dve.Fori(0, pairs) as i:
                for u in range(2):
                    dve.wait_ge(fetched[u], i * 16 + 16)
                    dve.wait_ge(*stored.before(i, u))
                    nc.vector.scalar_tensor_tensor(out[:, u, :], y[:, u, :], wcol[:, u, 0:1], base[:, u, :],
                                                   ALU.mult, ALU.add).then_inc(out_ready.sem, 1)



_INPUTS = {
    "x": "L0_attn_x", "w_attn": "L0_attn_W_attn", "b_attn": "L0_attn_b_attn", "w_proj": "L0_attn_W_proj",
    "b_proj": "L0_attn_b_proj", "wqkv": "L0_ffn_wqkv", "q_scale": "L0_ffn_q_scale", "k_scale": "L0_ffn_k_scale",
    "wo": "L0_ffn_wo", "ln_g": "L0_ffn_ln_g", "ln_b": "L0_ffn_ln_b", "w1": "L0_ffn_w1", "b1": "L0_ffn_b1",
    "w2": "L0_ffn_w2", "b2": "L0_ffn_b2", "w_in": "L1_attn_W_in", "conv_w": "L1_attn_conv_w",
    "conv_b": "L1_attn_conv_b", "w_x": "L1_attn_W_x", "w_dt": "L1_attn_W_dt", "b_dt": "L1_attn_b_dt",
    "a_log": "L1_attn_A_log", "d": "L1_attn_D", "w_out": "L1_attn_W_out", "w_router": "L1_ffn_w_router",
    "w_gate": "L1_ffn_w_gate", "w_up": "L1_ffn_w_up", "w_down": "L1_ffn_w_down",
}
_FLAT = {"x": (TOKENS, DIM), "w_gate": (EXPERTS * DIM, DIM), "w_up": (EXPERTS * DIM, DIM),
         "w_down": (EXPERTS * DIM, DIM)}
_BETWEEN = {
    "v": (SEQS * GROUPS * SEQ, GW), "yT": (SEQS * DIM, SEQ),
    "x1": (TOKENS, DIM), "z": (TOKENS + 1, DIM), "z1": (TOKENS + 1, DIM), "x2": (TOKENS, DIM),
    "xin": (SEQS * DI, SEQ), "sz": (SEQS * DI, SEQ), "bc": (SEQS * 2 * NS, SEQ), "xs": (SEQS * DI, SEQ),
    "ndt": (SEQS * DI, SEQ), "ndu": (SEQS * DI, SEQ), "ygT": (SEQS * DI, SEQ), "xt": (TOKENS, DIM),
    "base": (TOKENS, DIM), "chosen": (TOKENS, EXPERTS), "meta": (TOKENS, 2), "weight": (P, TILES),
    "slots_x": (SLOTS + TOKENS, DIM), "slots_y": (SLOTS, DIM),
}


def tables():
    return {"ident": np.eye(P, dtype=np.float32), "zeros": np.zeros((1, DIM), np.float32),
            **attention_tables(), **rope_tables(), **slot_tables()}


def build(nc, T):
    with nc.allow_non_contiguous_dma(reason="weights' columns, biases and slots, a few elements each"):
        phase_qkv(nc, T)
        phase_attention(nc, T)
        phase_project(nc, T)
        for layer in range(2):
            phase_window(nc, T, layer)
            phase_feed_forward(nc, T, layer, layer == 1)
        phase_in_projection(nc, T)
        phase_dt(nc, T)
        phase_scan(nc, T)
        phase_router(nc, T)
        phase_slots(nc, T)
        phase_scatter(nc, T)
        phase_experts(nc, T)
        phase_combine(nc, T)


def kernel(**inputs):
    import concourse.bacc as bacc
    from concourse.bass_utils import run_bass_kernel_spmd

    nc = bacc.Bacc("TRN2", target_bir_lowering=False, num_devices=1)
    arrays, T = {}, {}
    given = {name: np.ascontiguousarray(inputs[full]) for name, full in _INPUTS.items()}
    given = {name: a.reshape(_FLAT.get(name, a.shape)) for name, a in given.items()}
    for name, a in {**given, **tables()}.items():
        arrays[f"in_{name}"] = a
        T[name] = nc.dram_tensor(f"in_{name}", a.shape, mybir.dt.from_np(a.dtype), kind="ExternalInput").ap()
    for name, shape in _BETWEEN.items():
        T[name] = nc.dram_tensor(f"between_{name}", shape, F32, kind="Internal").ap()
    for name in ("q_parts", "k_parts"):
        T[name] = nc.dram_tensor(f"between_{name}", (3 * SEQS * DIM, SEQ), BF16, kind="Internal").ap()
    for name in ("slot_to", "slot_from"):
        T[name] = nc.dram_tensor(f"between_{name}", (P, TILES), I32, kind="Internal").ap()
    T["out"] = nc.dram_tensor("out_x", (TOKENS, DIM), F32, kind="ExternalOutput").ap()
    build(nc, T)
    result = run_bass_kernel_spmd(nc, [arrays], core_ids=[0])
    return result.results[0]["out_x"].reshape(SEQS, SEQ, DIM)
```
